# Optimizing a Trainium2 kernel written in Bass

```python
import numpy as np
import jax
import jax.numpy as jnp

def _softmax(x, axis=-1):
    return jax.nn.softmax(x, axis=axis)

def _gelu(x):
    return jax.nn.gelu(x, approximate=True)

def _silu(x):
    return jax.nn.silu(x)

def _sigmoid(x):
    return jax.nn.sigmoid(x)

def _layernorm(x, axis=-1, eps=1e-05):
    m = jnp.mean(x, axis=axis, keepdims=True)
    v = jnp.var(x, axis=axis, keepdims=True)
    return (x - m) / jnp.sqrt(v + eps)

def _scatter_add(tgt, idx, src, axis=0):
    return tgt.at[idx].add(src)

def _segment_sum(src, seg, n):
    return jax.ops.segment_sum(src, seg, n)
kernel_name = 'mk_gnn_ffn_d1_gnn_r8_b64d75'

def setup_inputs(seed: int=0):
    np.random.seed(seed)
    _w = jnp.asarray

    def _rec_inputs():
        import jax
        import jax.numpy as jnp
        _gk = jax.random.key(seed)
        x = -0.0002117 + 1 * jax.random.normal(jax.random.fold_in(_gk, 1), (12500, 256), jnp.float32)
        src = jax.random.randint(jax.random.fold_in(_gk, 2), (200000,), 0, 12500, jnp.int32)
        dst = jnp.minimum((12500 * jax.random.uniform(jax.random.fold_in(_gk, 3), (200000,)) ** 2.0).astype(jnp.int32), 99999)
        _o = jnp.argsort(dst, stable=True)
        src = src[_o]
        dst = dst[_o]
        return (x, src, dst)
    x, src, dst = _rec_inputs()

    def _L0_gnn_setup():
        import jax, jax.numpy as jnp
        import numpy as np
        N_NODES = 12500
        N_EDGES = 37500
        DIM = 256
        LN_EPS = 1e-05
        key = jax.random.key(seed)
        ks = jax.random.split(key, 4)
        scale = 1.0 / np.sqrt(DIM)
        h = jax.random.normal(ks[0], (N_NODES, DIM), dtype=jnp.float32)
        edge_index = jax.random.randint(ks[1], (2, N_EDGES), 0, N_NODES, dtype=jnp.int64)
        W1 = jax.random.normal(ks[2], (DIM, DIM), dtype=jnp.float32) * scale
        b1 = jnp.zeros((DIM,), dtype=jnp.float32)
        W2 = jax.random.normal(ks[3], (DIM, DIM), dtype=jnp.float32) * scale
        b2 = jnp.zeros((DIM,), dtype=jnp.float32)
        eps = jnp.zeros((), dtype=jnp.float32)
        gamma = jnp.ones((DIM,), dtype=jnp.float32)
        beta = jnp.zeros((DIM,), dtype=jnp.float32)
        return {'h': h, 'edge_index': edge_index, 'W1': W1, 'b1': b1, 'W2': W2, 'b2': b2, 'eps': eps, 'gamma': gamma, 'beta': beta}
    _L0_gnn_all = _L0_gnn_setup()
    _L0_gnn_in = {k: v for k, v in _L0_gnn_all.items() if k in ('W1', 'b1', 'W2', 'b2', 'eps', 'gamma', 'beta')}
    del _L0_gnn_all

    def _L0_ffn_setup():
        import jax, jax.numpy as jnp
        import numpy as np
        E = 8
        K = 2
        D = 256
        H = 512
        DOUT = 256
        EPS = 1e-05
        key = jax.random.key(seed)
        ks = jax.random.split(key, 9)
        s = 0.02
        return {'x': jax.random.normal(ks[0], (4, 1024, D), jnp.float32), 'gamma': 1.0 + 0.05 * jax.random.normal(ks[1], (D,), jnp.float32), 'beta': 0.05 * jax.random.normal(ks[2], (D,), jnp.float32), 'Wr': 0.01 * jax.random.normal(ks[3], (D, E), jnp.float32), 'br': jnp.zeros((E,), jnp.float32), 'W1': s * jax.random.normal(ks[4], (E, D, H), jnp.float32), 'b1': s * jax.random.normal(ks[5], (E, H), jnp.float32), 'W2': s * jax.random.normal(ks[6], (E, H, DOUT), jnp.float32), 'b2': s * jax.random.normal(ks[7], (E, DOUT), jnp.float32)}
    _L0_ffn_all = _L0_ffn_setup()
    _L0_ffn_in = {k: v for k, v in _L0_ffn_all.items() if k in ('gamma', 'beta', 'Wr', 'br', 'W1', 'b1', 'W2', 'b2')}
    del _L0_ffn_all
    return {'x': x, 'src': src, 'dst': dst, 'L0_gnn_W1': _L0_gnn_in['W1'], 'L0_gnn_b1': _L0_gnn_in['b1'], 'L0_gnn_W2': _L0_gnn_in['W2'], 'L0_gnn_b2': _L0_gnn_in['b2'], 'L0_gnn_eps': _L0_gnn_in['eps'], 'L0_gnn_gamma': _L0_gnn_in['gamma'], 'L0_gnn_beta': _L0_gnn_in['beta'], 'L0_ffn_gamma': _L0_ffn_in['gamma'], 'L0_ffn_beta': _L0_ffn_in['beta'], 'L0_ffn_Wr': _L0_ffn_in['Wr'], 'L0_ffn_br': _L0_ffn_in['br'], 'L0_ffn_W1': _L0_ffn_in['W1'], 'L0_ffn_b1': _L0_ffn_in['b1'], 'L0_ffn_W2': _L0_ffn_in['W2'], 'L0_ffn_b2': _L0_ffn_in['b2']}

def reference(x, src, dst, L0_gnn_W1, L0_gnn_b1, L0_gnn_W2, L0_gnn_b2, L0_gnn_eps, L0_gnn_gamma, L0_gnn_beta, L0_ffn_gamma, L0_ffn_beta, L0_ffn_Wr, L0_ffn_br, L0_ffn_W1, L0_ffn_b1, L0_ffn_W2, L0_ffn_b2):
    import jax
    import jax.numpy as jnp

    def _L0_gnn_ref(h, edge_index, W1, b1, W2, b2, eps, gamma, beta):
        import jax, jax.numpy as jnp
        import numpy as np
        N_NODES = 12500
        N_EDGES = 37500
        DIM = 256
        LN_EPS = 1e-05
        src, dst = (edge_index[0], edge_index[1])
        agg = jax.ops.segment_sum(h[src], dst, num_segments=h.shape[0])
        z = (1.0 + eps) * h + agg
        z = jax.nn.relu(z @ W1 + b1) @ W2 + b2
        r = z + h
        mu = jnp.mean(r, axis=-1, keepdims=True)
        var = jnp.mean(jnp.square(r - mu), axis=-1, keepdims=True)
        ln = (r - mu) * jax.lax.rsqrt(var + LN_EPS) * gamma + beta
        return jax.nn.relu(ln)

    def _L0_ffn_ref(x, gamma, beta, Wr, br, W1, b1, W2, b2):
        import jax, jax.numpy as jnp
        import numpy as np
        E = 8
        K = 2
        D = 256
        H = 512
        DOUT = 256
        EPS = 1e-05
        mu = jnp.mean(x, axis=-1, keepdims=True)
        var = jnp.mean(jnp.square(x - mu), axis=-1, keepdims=True)
        xn = (x - mu) * jax.lax.rsqrt(var + EPS) * gamma + beta
        logits = jnp.einsum('bsd,de->bse', xn, Wr) + br
        top_vals, top_idx = jax.lax.top_k(logits, K)
        w = jax.nn.softmax(top_vals, axis=-1)
        w_full = jnp.einsum('bsk,bske->bse', w, jax.nn.one_hot(top_idx, E, dtype=w.dtype))
        y = jnp.zeros(x.shape[:-1] + (DOUT,), x.dtype)
        for e in range(E):
            h = jax.nn.gelu(jnp.einsum('bsd,dh->bsh', xn, W1[e]) + b1[e], approximate=False)
            y_e = jnp.einsum('bsh,hd->bsd', h, W2[e]) + b2[e]
            y = y + y_e * w_full[..., e, None]
        return y
    edge_index = jnp.stack([src, dst])
    x = x + _L0_gnn_ref(_layernorm(x, axis=-1), edge_index, L0_gnn_W1, L0_gnn_b1, L0_gnn_W2, L0_gnn_b2, L0_gnn_eps, L0_gnn_gamma, L0_gnn_beta)
    x = x + _L0_ffn_ref(_layernorm(x, axis=-1)[None], L0_ffn_gamma, L0_ffn_beta, L0_ffn_Wr, L0_ffn_br, L0_ffn_W1, L0_ffn_b1, L0_ffn_W2, L0_ffn_b2)[0]
    return x

_drawn_inputs = setup_inputs


def setup_inputs(seed=0):
    import zlib

    import numpy as np

    out = dict(_drawn_inputs(seed))
    spreads = {'L0_gnn_b1': (0.0, 0.535),
     'L0_gnn_b2': (0.0, 0.386),
     'L0_gnn_gamma': (1.0, 0.2),
     'L0_gnn_beta': (0.0, 0.1),
     'L0_ffn_br': (0.0, 0.1)}
    factors = {'L0_ffn_gamma': 7.925, 'L0_ffn_beta': 6.835, 'L0_ffn_b1': 8.0, 'L0_ffn_b2': 5.793}
    for name, (base, spread) in spreads.items():
        noise = np.random.default_rng([zlib.crc32(name.encode()), seed]).standard_normal(out[name].shape)
        drawn = base * np.exp(spread * noise) if base else spread * noise
        out[name] = jnp.asarray(drawn.astype(out[name].dtype))
    for name, factor in factors.items():
        out[name] = (out[name] * factor).astype(out[name].dtype)
    return out
```

```python
from contextlib import ExitStack

import concourse.bass as bass
from concourse import mybir

F32, F16, I32, U32 = mybir.dt.float32, mybir.dt.float16, mybir.dt.int32, mybir.dt.uint32
ACT, ALU = mybir.ActivationFunctionType, mybir.AluOpType
AX_X = mybir.AxisListType.X

P = 128
D, KD = 256, 2
H, KH, E = 512, 4, 8
WPS = 4
STEPS = 25
WINDOWS = WPS * STEPS
ROWS = WINDOWS * P
EDGES = 200000
TILES = -(-EDGES // P)
TC = 13
TPAD = TC * P

NOWHERE = ROWS
U = 8
G = 4
TCOLS = TILES + U + 1
EPS = 1e-5
WSCALE = 64.0
CH = 10
RSQRT_SEED = float(0x5F3759DF)


def rsqrt(dve, chain, y, var, tmp):
    ve, hv, a = tmp
    dve.tensor_scalar(ve, var, EPS, None, ALU.add).then_inc(chain, 1)
    dve.wait_ge(chain, 1)
    dve.sem_inc(chain, -1)
    dve.tensor_scalar(hv, ve, -0.5, None, ALU.mult)
    dve.tensor_scalar(a.bitcast(I32), ve.bitcast(I32), 1, None, ALU.logical_shift_right).then_inc(chain, 1)
    dve.wait_ge(chain, 1)
    dve.sem_inc(chain, -1)
    dve.tensor_scalar(y.bitcast(I32), a.bitcast(I32), -1.0, RSQRT_SEED, ALU.mult, ALU.add).then_inc(chain, 1)
    dve.wait_ge(chain, 1)
    dve.sem_inc(chain, -1)
    for _ in range(3):
        dve.tensor_tensor(a, y, y, ALU.mult).then_inc(chain, 1)
        dve.wait_ge(chain, 1)
        dve.sem_inc(chain, -1)
        dve.tensor_tensor(a, a, hv, ALU.mult).then_inc(chain, 1)
        dve.wait_ge(chain, 1)
        dve.sem_inc(chain, -1)
        dve.scalar_tensor_tensor(out=y, in0=a, scalar=1.5, in1=y, op0=ALU.add, op1=ALU.mult).then_inc(chain, 1)
        dve.wait_ge(chain, 1)
        dve.sem_inc(chain, -1)


def gnn_moe_kernel(nc, x, src_cols, dst_cols, dst_rows, gW1, gb1, gW2, gb2, geps, ggamma, gbeta,
                   fgamma, fbeta, fWr, fbr, fW1, fb1, fW2, fb2, out):
    table = nc.dram_tensor("normed_rows", (ROWS, 2 * D), F16, kind="Internal").ap()
    with ExitStack() as ctx:
        def sb(name, shape, dt=F32):
            return ctx.enter_context(nc.sbuf_tensor(name, shape, dt))

        def sem(name):
            return ctx.enter_context(nc.semaphore(name))

        psum = ctx.enter_context(nc.psum_tensor("psum", [P, 8, 512], F32))
        src_idx = sb("src_idx", [P, TCOLS], I32)
        dst_f = sb("dst_f", [P, TCOLS])
        rstd0 = sb("rstd0", [P, WINDOWS])
        shift0 = sb("shift0", [P, WINDOWS])
        lo_row = sb("lo_row", [1, 128], I32)
        nb_row = sb("nb_row", [1, 128], I32)
        rounds = sb("rounds", [1, 8], I32)
        base = sb("base", [P, WINDOWS])
        ident = sb("ident", [P, P])
        iota16 = sb("iota16", [P, P], F16)
        iota8 = sb("iota8", [P, 8])
        zeros16 = sb("zeros16", [P, 512], F16)
        gW1s, gW2s = sb("gW1s", [P, KD, D]), sb("gW2s", [P, KD, D])
        gb1s = sb("gb1s", [P, KD])
        gb2s, ggs, gbs = sb("gb2s", [P, D]), sb("ggs", [P, D]), sb("gbs", [P, D])
        eps1 = sb("eps1", [P, 1])
        fgs, fbs = sb("fgs", [P, KD]), sb("fbs", [P, KD])
        fWrs, fbrs = sb("fWrs", [P, KD, E]), sb("fbrs", [P, E])
        fb1s = sb("fb1s", [P, E * KH])
        fb2s = sb("fb2s", [E, D])
        small = sb("small", [P, 5, CH])
        iota_k = sb("iota_k", [P, 2, P])

        chain = sem("chain")
        const_in = sem("const_in")
        edges_in = sem("edges_in")

        with ExitStack() as first:
            def fsb(name, shape, dt=F32):
                return first.enter_context(nc.sbuf_tensor(name, shape, dt))

            xin = [fsb(f"xin{s}", [P, CH, D]) for s in range(2)]
            h32 = [fsb(f"h32_{s}", [P, CH, D]) for s in range(2)]
            pair = [fsb(f"pair{s}", [P, CH, 2 * D], F16) for s in range(2)]
            stats = fsb("stats", [P, CH, 6])
            mv = fsb("mv", [P, CH, 2])
            dst_i = fsb("dst_i", [P, TCOLS], I32)
            rows_i = fsb("rows_i", [P, TC, P], I32)
            tmin, tmax = fsb("tmin", [P, TC]), fsb("tmax", [P, TC])
            base_end = fsb("base_end", [P, WINDOWS])
            tnum_i = fsb("tnum_i", [P, TC], I32)
            tnum = fsb("tnum", [P, 2, TC])
            base_i = fsb("base_i", [P, WINDOWS], I32)
            iota_i = fsb("iota_i", [P, P], I32)
            m1 = fsb("m1", [P, TC, WINDOWS])
            m2 = fsb("m2", [P, TC, WINDOWS])
            ends = fsb("ends", [P, 2, WINDOWS])
            ends_k = fsb("ends_k", [P, 2])
            lo_k, nt_k = fsb("lo_k", [P, 1]), fsb("nt_k", [P, 1])
            row_f = fsb("row_f", [1, 2, WINDOWS])
            total = fsb("total", [1, 1])

            x_in = [first.enter_context(nc.semaphore(f"x_in{s}")) for s in range(2)]
            pair_out = [first.enter_context(nc.semaphore(f"pair_out{s}")) for s in range(2)]
            x_free, stats_ready, h_ready, pair_ready = (
                first.enter_context(nc.semaphore(n)) for n in ("x_free", "stats_ready", "h_ready", "pair_ready"))
            h_free, pool_const, pool_chain = (
                first.enter_context(nc.semaphore(n)) for n in ("h_free", "pool_const", "pool_chain"))
            ends_ready, ends_turned, cols_ready, cols_turned = (
                first.enter_context(nc.semaphore(n)) for n in ("ends_ready", "ends_turned", "cols_ready", "cols_turned"))
            ident_ready = first.enter_context(nc.semaphore("ident_ready"))
            act_chain = first.enter_context(nc.semaphore("act_chain0"))
            block = first.enter_context(nc.Block())
            CHUNKS = WINDOWS // CH
            x_chunk = x.rearrange("(c i p) d -> c p i d", i=CH, p=P)
            table_chunk = table.rearrange("(c i p) d -> c p i d", i=CH, p=P)

            @block.sync
            def _(sp):
                for s in range(2):
                    sp.dma_start(xin[s][:], x_chunk[s]).then_inc(x_in[s], 16)
                for dst, source in ((rows_i[:], dst_rows.rearrange("(c p) e -> p c e", p=P)), (dst_i[:], dst_cols),
                                    (src_idx[:], src_cols)):
                    sp.dma_start(dst, source).then_inc(edges_in, 16)

                def turn(c, s, last):
                    sp.wait_ge(pair_ready, 1)
                    sp.sem_inc(pair_ready, -1)
                    sp.dma_start(table_chunk[c], pair[s][:]).then_inc(pair_out[s], 16)
                    if not last:
                        sp.wait_ge(x_free, 1)
                        sp.sem_inc(x_free, -1)
                        sp.dma_start(xin[s][:], x_chunk[c + 2]).then_inc(x_in[s], 16)

                with sp.Fori(0, CHUNKS // 2 - 1) as i:
                    for s in range(2):
                        turn(2 * i + s, s, False)
                for s in range(2):
                    turn(CHUNKS - 2 + s, s, True)

            @block.gpsimd
            def _(pool):
                pool.memset(ident[:], 0.0).then_inc(pool_chain, 1)
                pool.wait_ge(pool_chain, 1)
                pool.sem_inc(pool_chain, -1)
                pool.affine_select(out=ident[:], in_=ident[:], compare_op=ALU.not_equal, fill=1.0, base=0,
                                   pattern=[[-1, P]], channel_multiplier=1).then_inc(ident_ready, 1)
                pool.iota(tnum_i[:], pattern=[[P, TC]], base=0, channel_multiplier=1)
                pool.iota(base_i[:], pattern=[[-P, STEPS], [STEPS * P, WPS]], base=(STEPS - 1) * P,
                          channel_multiplier=0)
                pool.iota(iota_i[:], pattern=[[1, P]], base=0, channel_multiplier=0)
                pool.memset(zeros16[:], 0.0)
                pool.memset(lo_row[:], 0)
                pool.memset(nb_row[:], 1 << 20).then_inc(pool_const, 1)

                def split(s, first_turn):
                    pool.wait_ge(h_ready, 1)
                    pool.sem_inc(h_ready, -1)
                    if not first_turn:
                        pool.wait_ge(pair_out[s], 16)
                        pool.sem_inc(pair_out[s], -16)
                    pool.tensor_copy(pair[s][:, :, 0:D], h32[s][:]).then_inc(pool_chain, 1)
                    pool.wait_ge(pool_chain, 1)
                    pool.sem_inc(pool_chain, -1)
                    pool.tensor_tensor(pair[s][:, :, D:2 * D], h32[s][:], pair[s][:, :, 0:D], ALU.subtract)\
                        .then_inc(pool_chain, 1)
                    pool.wait_ge(pool_chain, 1)
                    pool.sem_inc(pool_chain, -1)
                    pool.sem_inc(pair_ready, 1)
                    pool.sem_inc(h_free, 1)

                for s in range(2):
                    split(s, True)
                with pool.Fori(0, CHUNKS // 2 - 1):
                    for s in range(2):
                        split(s, False)
                for s in range(2):
                    pool.wait_ge(pair_out[s], 16)
                    pool.sem_inc(pair_out[s], -16)

            @block.scalar
            def _(act):
                with nc.allow_non_contiguous_dma(reason="small constants, once"):
                    loads = [
                        (gW1s[:], gW1.rearrange("(k p) n -> p k n", p=P)), (gW2s[:], gW2.rearrange("(k p) n -> p k n", p=P)),
                        (gb1s[:], gb1.rearrange("(k p) -> p k", p=P)),
                        (gb2s[:], gb2.partition_broadcast(P)), (ggs[:], ggamma.partition_broadcast(P)),
                        (gbs[:], gbeta.partition_broadcast(P)), (eps1[:], geps.partition_broadcast(P)),
                        (fgs[:], fgamma.rearrange("(k p) -> p k", p=P)), (fbs[:], fbeta.rearrange("(k p) -> p k", p=P)),
                        (fWrs[:], fWr.rearrange("(k p) e -> p k e", p=P)), (fbrs[:], fbr.partition_broadcast(P)),
                        (fb1s[:], fb1.rearrange("e (j p) -> p (e j)", p=P)), (fb2s[:], fb2),
                    ]
                    for dst, source in loads:
                        act.dma_start(dst, source).then_inc(const_in, 16)

                def norm(c, s):
                    act.wait_ge(stats_ready, 1)
                    act.sem_inc(stats_ready, -1)
                    act.wait_ge(h_free, 1)
                    act.sem_inc(h_free, -1)
                    for i in range(CH):
                        w = c * CH + i
                        ins = act.activation(h32[s][:, i, :], xin[s][:, i, :], ACT.Identity,
                                             bias=shift0[:, bass.ds(w, 1)], scale=rstd0[:, bass.ds(w, 1)])
                    ins.then_inc(act_chain, 1)
                    act.wait_ge(act_chain, 1)
                    act.sem_inc(act_chain, -1)
                    act.sem_inc(h_ready, 1)
                    act.sem_inc(x_free, 1)

                act.sem_inc(h_free, 2)
                with act.Fori(0, CHUNKS // 2) as i:
                    for s in range(2):
                        norm(2 * i + s, s)
                act.wait_ge(const_in, 16 * len(loads))

            @block.vector
            def _(dve):
                def moments(c, s):
                    dve.wait_ge(x_in[s], 16)
                    dve.sem_inc(x_in[s], -16)
                    for i in range(CH):
                        ins = dve.bn_stats(stats[:, i, :], xin[s][:, i, :])
                    ins.then_inc(chain, 1)
                    dve.wait_ge(chain, 1)
                    dve.sem_inc(chain, -1)
                    for i in range(CH):
                        ins = dve.bn_aggr(mv[:, i, :], stats[:, i, :])
                    ins.then_inc(chain, 1)
                    dve.wait_ge(chain, 1)
                    dve.sem_inc(chain, -1)
                    col = bass.ds(c * CH, CH)
                    rsqrt(dve, chain, small[:, 3, 0:CH], mv[:, :, 1], [small[:, n, 0:CH] for n in range(3)])
                    dve.tensor_copy(rstd0[:, col], small[:, 3, 0:CH])
                    dve.scalar_tensor_tensor(out=shift0[:, col], in0=mv[:, :, 0], scalar=-1.0,
                                             in1=small[:, 3, 0:CH], op0=ALU.mult, op1=ALU.mult).then_inc(chain, 1)
                    dve.wait_ge(chain, 1)
                    dve.sem_inc(chain, -1)
                    dve.sem_inc(stats_ready, 1)

                with dve.Fori(0, CHUNKS // 2) as i:
                    for s in range(2):
                        moments(2 * i + s, s)

                dve.wait_ge(pool_const, 1)
                dve.sem_inc(pool_const, -1)
                dve.wait_ge(edges_in, 48)
                dve.tensor_copy(dst_f[:], dst_i[:])
                dve.tensor_copy(base[:], base_i[:])
                dve.tensor_scalar(base_end[:], base_i[:], float(P - 1), None, ALU.add)
                dve.tensor_copy(iota16[:], iota_i[:])
                dve.tensor_copy(iota8[:], iota_i[:, 0:8])
                dve.tensor_scalar(tnum[:, 0, :], tnum_i[:], 1.0, None, ALU.add)
                dve.tensor_scalar(tnum[:, 1, :], tnum_i[:], -1.0, float(TILES), ALU.mult, ALU.add)
                dve.tensor_reduce(tmin[:], rows_i[:], AX_X, ALU.min)
                dve.tensor_reduce(tmax[:], rows_i[:], AX_X, ALU.max).then_inc(chain, 1)
                dve.wait_ge(chain, 1)
                dve.sem_inc(chain, -1)

                def over_k(a):
                    return a.unsqueeze(2).broadcast_to([P, TC, WINDOWS])

                def over_t(a):
                    return a.unsqueeze(1).broadcast_to([P, TC, WINDOWS])

                dve.tensor_tensor(m1[:], over_t(base[:]), over_k(tmax[:]), ALU.is_le)
                dve.tensor_tensor(m2[:], over_t(base_end[:]), over_k(tmin[:]), ALU.is_ge).then_inc(chain, 1)
                dve.wait_ge(chain, 1)
                dve.sem_inc(chain, -1)
                dve.tensor_tensor(m1[:], m1[:], m2[:], ALU.mult).then_inc(chain, 1)
                dve.wait_ge(chain, 1)
                dve.sem_inc(chain, -1)
                for n in range(2):
                    dve.tensor_tensor(m2[:], m1[:], over_k(tnum[:, n, :]), ALU.mult).then_inc(chain, 1)
                    dve.wait_ge(chain, 1)
                    dve.sem_inc(chain, -1)
                    dve.tensor_reduce(ends[:, n, :], m2[:].rearrange("p c k -> p k c"), AX_X, ALU.max).then_inc(chain, 1)
                    dve.wait_ge(chain, 1)
                    dve.sem_inc(chain, -1)
                dve.sem_inc(ends_ready, 1)
                dve.wait_ge(ends_turned, 1)
                dve.sem_inc(ends_turned, -1)
                turned = psum[0:WINDOWS, 0, 0:2 * P].rearrange("k (n p) -> k n p", n=2)
                dve.tensor_reduce(ends_k[0:WINDOWS, :], turned, AX_X, ALU.max).then_inc(chain, 1)
                dve.wait_ge(chain, 1)
                dve.sem_inc(chain, -1)
                dve.tensor_scalar(lo_k[0:WINDOWS, :], ends_k[0:WINDOWS, 1:2], -1.0, float(TILES),
                                  ALU.mult, ALU.add).then_inc(chain, 1)
                dve.wait_ge(chain, 1)
                dve.sem_inc(chain, -1)
                dve.tensor_scalar(lo_k[0:WINDOWS, :], lo_k[0:WINDOWS, :], float(TILES - 1), None, ALU.min).then_inc(chain, 1)
                dve.wait_ge(chain, 1)
                dve.sem_inc(chain, -1)
                dve.tensor_tensor(nt_k[0:WINDOWS, :], ends_k[0:WINDOWS, 0:1], lo_k[0:WINDOWS, :],
                                  ALU.subtract).then_inc(chain, 1)
                dve.wait_ge(chain, 1)
                dve.sem_inc(chain, -1)
                dve.tensor_scalar(nt_k[0:WINDOWS, :], nt_k[0:WINDOWS, :], 1.0, float(U - 1),
                                  ALU.max, ALU.add).then_inc(chain, 1)
                dve.wait_ge(chain, 1)
                dve.sem_inc(chain, -1)
                dve.sem_inc(cols_ready, 1)
                dve.wait_ge(cols_turned, 1)
                dve.sem_inc(cols_turned, -1)
                dve.tensor_copy(lo_row[:, 0:WINDOWS], psum[0:1, 1, 0:WINDOWS])
                dve.tensor_copy(nb_row[:, 0:WINDOWS], psum[0:1, 1, P:P + WINDOWS]).then_inc(chain, 1)
                dve.wait_ge(chain, 1)
                dve.sem_inc(chain, -1)
                dve.tensor_scalar(nb_row[:, 0:WINDOWS], nb_row[:, 0:WINDOWS], U.bit_length() - 1, None,
                                  ALU.logical_shift_right).then_inc(chain, 1)
                dve.wait_ge(chain, 1)
                dve.sem_inc(chain, -1)
                dve.tensor_copy(row_f[:, 0, :], nb_row[:, 0:WINDOWS]).then_inc(chain, 1)
                dve.wait_ge(chain, 1)
                dve.sem_inc(chain, -1)
                dve.tensor_reduce(total[:], row_f[:, 0, :], AX_X, ALU.add).then_inc(chain, 1)
                dve.wait_ge(chain, 1)
                dve.sem_inc(chain, -1)
                dve.tensor_scalar(rounds[:, 0:1], total[:], float(G - 1), None, ALU.add).then_inc(chain, 1)
                dve.wait_ge(chain, 1)
                dve.sem_inc(chain, -1)
                dve.tensor_scalar(rounds[:, 1:2], rounds[:, 0:1], G.bit_length() - 1, None,
                                  ALU.logical_shift_right).then_inc(chain, 1)
                dve.wait_ge(chain, 1)
                dve.sem_inc(chain, -1)

            @block.tensor
            def _(pe):
                pe.wait_ge(ident_ready, 1)
                pe.sem_inc(ident_ready, -1)
                pe.wait_ge(ends_ready, 1)
                pe.sem_inc(ends_ready, -1)
                for n in range(2):
                    ins = pe.transpose(psum[0:WINDOWS, 0, n * P:(n + 1) * P], ends[:, n, :], ident[:])
                ins.then_inc(ends_turned, 1)
                pe.wait_ge(cols_ready, 1)
                pe.sem_inc(cols_ready, -1)
                for n, col in enumerate((lo_k, nt_k)):
                    ins = pe.transpose(psum[0:1, 1, n * P:n * P + WINDOWS], col[0:WINDOWS, :],
                                       ident[0:WINDOWS, 0:WINDOWS])
                ins.then_inc(cols_turned, 1)

        ring = sb("ring", [P, G * U * 2 * D], F16)
        idx_now = sb("idx_now", [P, G, U], I32)
        onehot = sb("onehot", [P, G * U * P], F16)
        w1hi, w1lo = sb("w1hi", [P, E, KD, H], F16), sb("w1lo", [P, E, KD, H], F16)
        w2hi, w2lo = sb("w2hi", [P, E, KH, D], F16), sb("w2lo", [P, E, KH, D], F16)
        b2s = sb("b2s", [E, D])
        xw = [sb(f"xw{s}", [P, WPS, D]) for s in range(2)]
        hw = sb("hw", [P, WPS, D])
        z = sb("z", [P, WPS, D])
        zT = sb("zT", [P, KD, 2 * P])
        aT = [sb(f"aT{p}", [P, KD, 2 * P]) for p in range(2)]
        r = sb("r", [P, WPS, D])
        t = sb("t", [P, WPS, D])
        bstats = sb("bstats", [P, WPS, 6])
        bmv = sb("bmv", [P, WPS, 2])
        opeps = sb("opeps", [P, 1])
        xT32 = sb("xT32", [P, KD, WPS * P])
        xThi = [sb(f"xThi{s}", [P, KD, WPS * P], F16) for s in range(2)]
        xTlo = [sb(f"xTlo{s}", [P, KD, WPS * P], F16) for s in range(2)]
        logit = sb("logit", [P, WPS, E])
        top = sb("top", [P, WPS, 8])
        top_i = sb("top_i", [P, WPS, 8], U32)
        top_f = sb("top_f", [P, WPS, 8])
        gap = sb("gap", [P, WPS])
        tanh = sb("tanh", [P, WPS])
        wtop = sb("wtop", [P, 2, WPS])
        wsel = sb("wsel", [P, WPS, E])
        wf = [sb(f"wf{s}", [P, WPS, E]) for s in range(2)]
        wfT = zT[0:E].rearrange("e k n -> e (k n)")
        y = [sb(f"y{s}", [P, WPS, D]) for s in range(2)]
        g32 = sb("g32", [P, 4, WPS * P])
        hid_hi = [sb(f"hid_hi{s}", [P, KH, WPS * P], F16) for s in range(2)]
        hid_lo = [sb(f"hid_lo{s}", [P, KH, WPS * P], F16) for s in range(2)]
        prime = sb("prime", [1, 2, 16])

        def agg(b):
            return psum[:, b, :]

        def f1(c):
            return psum[:, 2 + c % 2, :]

        def f2(tb):
            return psum[:, 4 + tb % 2, 0:D]

        mA, mB = psum[:, 6, :], psum[:, 7, :]

        landed = [sem(f"landed{g}") for g in range(G)]
        batch_ready = sem("batch_ready")
        batch_used = sem("batch_used")
        onehot_free = sem("onehot_free")
        onehot_ready = sem("onehot_ready")
        x_loaded = sem("x_loaded")
        xw_free = sem("xw_free")
        hw_free = sem("hw_free")
        hw_ready = sem("hw_ready")
        agg_ready = sem("agg_ready")
        z_ready = sem("z_ready")
        z_free = sem("z_free")
        mA_free = sem("mA_free")
        mB_free = sem("mB_free")
        to_act = sem("to_act")
        to_dve = sem("to_dve")
        zT_ready = sem("zT_ready")
        aT_ready = sem("aT_ready")
        xn_ready = sem("xn_ready")
        xT_for_dve = sem("xT_for_dve")
        xT_for_pe = sem("xT_for_pe")
        xlo_ready = sem("xlo_ready")
        gap_ready = sem("gap_ready")
        tanh_ready = sem("tanh_ready")
        wf_ready = sem("wf_ready")
        wfT_ready = sem("wfT_ready")
        f1_ready = sem("f1_ready")
        f1_free = sem("f1_free")
        g_ready = sem("g_ready")
        g_free = sem("g_free")
        hid_free = sem("hid_free")
        lo_ready = sem("lo_ready")
        f2_ready = sem("f2_ready")
        f2_free = sem("f2_free")
        y_free = sem("y_free")
        y_done = sem("y_done")
        dev_ready = sem("dev_ready")
        applied = sem("applied")
        act_chain = sem("act_chain")
        pool_step = sem("pool_step")
        w_hi = sem("w_hi")
        stage_free = sem("stage_free")
        pe_chain = sem("pe_chain")
        opeps_ready = sem("opeps_ready")
        x_dma = [sem(f"x_dma{s}") for s in range(2)]
        out_dma = [sem(f"out_dma{s}") for s in range(2)]
        w_dma = [sem(f"w_dma{s}") for s in range(2)]
        x_step = x.rearrange("(i a p) d -> a p i d", i=WPS, p=P)
        out_step = out.rearrange("(i a p) d -> a p i d", i=WPS, p=P)
        rstd_step = rstd0[:].rearrange("p (i a) -> p i a", i=WPS)
        shift_step = shift0[:].rearrange("p (i a) -> p i a", i=WPS)
        block = ctx.enter_context(nc.Block())

        def steps(eng, first_step, body, ffn_only):
            first_step()
            with eng.Fori(0, (STEPS - 3) // 2) as j:
                for u in range(2):
                    body(2 * j + 1 + u, u, False)
            body(STEPS - 2, 0, False)
            body(STEPS - 1, 1, True)
            ffn_only()

        @block.gpsimd
        def _(pool):
            pool.wait_ge(edges_in, 48)
            n_rounds = pool.value_load(rounds[0:1, 1:2], min_val=1, max_val=1 << 20)
            k, tile, left = (pool.alloc_register(n) for n in ("window", "tile", "left"))
            pool.reg_mov(k, 0)
            pool.reg_load(tile, lo_row[0:1, 0:1])
            pool.reg_load(left, nb_row[0:1, 0:1])
            pool.sem_inc(batch_used, G)
            with pool.Fori(0, n_rounds):
                for g in range(G):
                    with pool.If(pool.snap(left) <= 0):
                        pool.reg_add(k, k, 1)
                        at = pool.snap(k, min_val=0, max_val=WINDOWS + 1)
                        pool.reg_load(tile, lo_row[0:1, bass.ds(at, 1)])
                        pool.reg_load(left, nb_row[0:1, bass.ds(at, 1)])
                        pool.nop()
                    pool.wait_ge(batch_used, 1)
                    pool.sem_inc(batch_used, -1)
                    pool.sem_inc(onehot_free, 1)
                    at = pool.snap(tile, min_val=0, max_val=TCOLS - U)
                    pool.tensor_copy(idx_now[:, g, :], src_idx[:, bass.ds(at, U)]).then_inc(pool_step, 1)
                    pool.wait_ge(pool_step, 1)
                    pool.sem_inc(pool_step, -1)
                    for j in range(U):
                        pool.indirect_dma_start(
                            ring[:, (g * U + j) * 2 * D:(g * U + j + 1) * 2 * D], None, table,
                            bass.IndirectOffsetOnAxis(ap=idx_now[:, g, j:j + 1], axis=0)).then_inc(landed[g], 16)
                    pool.reg_add(tile, tile, U)
                    pool.reg_add(left, left, -1)

        @block.sync
        def _(sp):
            n_rounds = sp.value_load(rounds[0:1, 1:2], min_val=1, max_val=1 << 20)
            with sp.Fori(0, n_rounds) as n:
                for g in range(G):
                    sp.wait_ge(landed[g], (n + 1) * (16 * U))
                    sp.wait_ge(onehot_ready, 1)
                    sp.sem_inc(onehot_ready, -1)
                    sp.sem_inc(batch_ready, 1)

        @block.tensor
        def _(pe):
            place = pe.alloc_register("place")
            pe.reg_mov(place, 0)

            def sum_edges(k, bank):
                nb = pe.value_load(nb_row[0:1, bass.ds(k, 1)], min_val=1, max_val=1 << 20)
                pe.matmul(agg(bank), zeros16[:, 0:P], zeros16[:], start=True, stop=False)
                with pe.Fori(0, nb):
                    pe.wait_ge(batch_ready, 1)
                    pe.sem_inc(batch_ready, -1)
                    at = pe.snap(place, min_val=0, max_val=(G - 1) * U * P)
                    row = pe.snap(at * (2 * D // P))
                    for j in range(U):
                        ins = pe.matmul(agg(bank), onehot[:, bass.ds(at + j * P, P)],
                                        ring[:, bass.ds(row + j * 2 * D, 2 * D)], start=False, stop=False)
                    ins.then_inc(batch_used, 1)
                    pe.reg_add(place, place, U * P)
                    pe.reg_alu(place, place, G * U * P - 1, ALU.bitwise_and)
                pe.matmul(agg(bank), zeros16[:, 0:P], zeros16[:], start=False, stop=True).then_inc(agg_ready, 1)

            def turn_z(p, bank, free):
                pe.wait_ge(z_ready, 1 if p == 0 else 2)
                pe.sem_inc(z_ready, -(1 if p == 0 else 2))
                pe.wait_ge(free, 1)
                pe.sem_inc(free, -1)
                for k in range(KD):
                    for i in range(2):
                        ins = pe.transpose(bank[:, k * D + i * P:k * D + (i + 1) * P],
                                           z[:, 2 * p + i, k * P:(k + 1) * P], ident[:])
                ins.then_inc(pe_chain, 1)
                pe.wait_ge(pe_chain, 1)
                pe.sem_inc(pe_chain, -1)
                pe.sem_inc(to_act, 1)
                pe.sem_inc(z_free, 1)

            def gnn1(p, bank, free):
                pe.wait_ge(zT_ready, 1)
                pe.sem_inc(zT_ready, -1)
                pe.wait_ge(free, 1)
                pe.sem_inc(free, -1)
                for j in range(KD):
                    for k in range(KD):
                        ins = pe.matmul(bank[:, j * D:(j + 1) * D], gW1s[:, k, j * P:(j + 1) * P], zT[:, k, :],
                                        start=(k == 0), stop=(k == KD - 1))
                ins.then_inc(to_act, 1)

            def gnn2(p, bank, free):
                pe.wait_ge(aT_ready, 1)
                pe.sem_inc(aT_ready, -1)
                pe.wait_ge(free, 1)
                pe.sem_inc(free, -1)
                for i in range(2):
                    for k in range(KD):
                        ins = pe.matmul(bank[:, i * D:(i + 1) * D], aT[p][:, k, i * P:(i + 1) * P], gW2s[:, k, :],
                                        start=(k == 0), stop=(k == KD - 1))
                ins.then_inc(to_dve, 1)

            def turn_x(p, bank, free):
                if p == 0:
                    pe.wait_ge(xn_ready, 1)
                    pe.sem_inc(xn_ready, -1)
                pe.wait_ge(free, 1)
                pe.sem_inc(free, -1)
                for k in range(KD):
                    for i in range(2):
                        ins = pe.transpose(bank[:, k * D + i * P:k * D + (i + 1) * P],
                                           r[:, 2 * p + i, k * P:(k + 1) * P], ident[:])
                ins.then_inc(to_act, 1)

            def route(s):
                pe.wait_ge(xT_for_pe, 2)
                pe.sem_inc(xT_for_pe, -2)
                pe.wait_ge(mA_free, 1)
                pe.sem_inc(mA_free, -1)
                for i in range(WPS):
                    for k in range(KD):
                        ins = pe.matmul(mA[:, i * E:(i + 1) * E], xT32[:, k, i * P:(i + 1) * P], fWrs[:, k, :],
                                        start=(k == 0), stop=(k == KD - 1))
                ins.then_inc(to_dve, 1)

            def turn_w(s):
                pe.wait_ge(wf_ready, 1)
                pe.sem_inc(wf_ready, -1)
                pe.wait_ge(mB_free, 1)
                pe.sem_inc(mB_free, -1)
                for i in range(WPS):
                    ins = pe.transpose(mB[0:E, i * P:(i + 1) * P], wf[s][:, i, :], ident[:])
                ins.then_inc(to_dve, 1)

            def out_bias(p, bank, free):
                if p == 0:
                    pe.wait_ge(wfT_ready, 1)
                    pe.sem_inc(wfT_ready, -1)
                pe.wait_ge(free, 1)
                pe.sem_inc(free, -1)
                for i in range(2):
                    ins = pe.matmul(bank[:, i * D:(i + 1) * D], wfT[:, (2 * p + i) * P:(2 * p + i + 1) * P], b2s[:],
                                    start=True, stop=True)
                ins.then_inc(to_dve, 1)

            def expert_in(e, c, s):
                if e == 0 and c == 0:
                    pe.wait_ge(xlo_ready, 2)
                    pe.sem_inc(xlo_ready, -2)
                pe.wait_ge(f1_free, 1)
                pe.sem_inc(f1_free, -1)
                n = 0
                for k in range(KD):
                    for w, v in ((w1hi, xThi), (w1lo, xThi), (w1hi, xTlo)):
                        ins = pe.matmul(f1(c), w[:, e, k, c * P:(c + 1) * P], v[s][:, k, :],
                                        start=(n == 0), stop=(n == 3 * KD - 1))
                        n += 1
                ins.then_inc(f1_ready, 1)

            def expert_out(e, tb):
                if tb == 0:
                    pe.wait_ge(lo_ready, KH)
                    pe.sem_inc(lo_ready, -KH)
                    pe.sem_inc(g_free, KH)
                pe.wait_ge(f2_free, 1)
                pe.sem_inc(f2_free, -1)
                cols = slice(tb * P, (tb + 1) * P)
                n = 0
                for k in range(KH):
                    for v, w in ((hid_hi, w2hi), (hid_hi, w2lo), (hid_lo, w2hi)):
                        ins = pe.matmul(f2(tb), v[e % 2][:, k, cols], w[:, e, k, :],
                                        start=(n == 0), stop=(n == 3 * KH - 1))
                        n += 1
                ins.then_inc(f2_ready, 1)

            def first_step():
                pe.wait_ge(opeps_ready, 1)
                pe.sem_inc(opeps_ready, -1)
                pe.sem_inc(mA_free, 1)
                pe.sem_inc(mB_free, 1)
                sum_edges(0, 0)
                sum_edges(1, 1)
                pe.wait_ge(z_ready, 1)
                pe.sem_inc(z_ready, -1)
                sum_edges(2, 0)
                turn_z(0, mA, mA_free)
                gnn1(0, mA, mA_free)
                gnn2(0, mA, mA_free)
                sum_edges(3, 1)
                turn_z(1, mB, mB_free)
                gnn1(1, mB, mB_free)
                gnn2(1, mB, mB_free)
                sum_edges(4, 0)
                sum_edges(5, 1)
                turn_x(0, mA, mA_free)
                turn_x(1, mB, mB_free)

            def body(b, s, last):
                for e in range(E + 1):
                    for c in range(KH):
                        if e < E:
                            expert_in(e, c, s)
                        if e > 0:
                            expert_out(e - 1, c)
                        if (e, c) == (0, 0):
                            route(s)
                        if (e, c) == (0, 1):
                            pe.wait_ge(z_ready, 1)
                            pe.sem_inc(z_ready, -1)
                            sum_edges(4 * b + 2, 0)
                        if (e, c) == (0, 2):
                            turn_w(s)
                        if (e, c) == (0, 3):
                            out_bias(0, mA, mA_free)
                            out_bias(1, mB, mB_free)
                        if (e, c) == (1, 0):
                            turn_z(0, mA, mA_free)
                        if (e, c) == (1, 1):
                            gnn1(0, mA, mA_free)
                        if (e, c) == (1, 2):
                            sum_edges(4 * b + 3, 1)
                        if (e, c) == (1, 3):
                            gnn2(0, mA, mA_free)
                        if (e, c) == (2, 0):
                            turn_z(1, mB, mB_free)
                        if (e, c) == (2, 1):
                            gnn1(1, mB, mB_free)
                        if (e, c) == (2, 3):
                            gnn2(1, mB, mB_free)
                        if (e, c) == (4, 0) and not last:
                            sum_edges(4 * b + 4, 0)
                        if (e, c) == (6, 0) and not last:
                            sum_edges(4 * b + 5, 1)
                        if (e, c) == (7, 0):
                            turn_x(0, mA, mA_free)
                        if (e, c) == (7, 1):
                            turn_x(1, mB, mB_free)

            def ffn_only():
                s = (STEPS - 1) % 2
                for e in range(E + 1):
                    for c in range(KH):
                        if e < E:
                            expert_in(e, c, s)
                        if e > 0:
                            expert_out(e - 1, c)
                        if (e, c) == (0, 0):
                            route(s)
                        if (e, c) == (0, 2):
                            turn_w(s)
                        if (e, c) == (0, 3):
                            out_bias(0, mA, mA_free)
                            out_bias(1, mB, mB_free)

            steps(pe, first_step, body, ffn_only)

        @block.scalar
        def _(act):
            w_pieces = [(fW1[e].rearrange("(k p) h -> p k h", p=P), KD) for e in range(E)] + \
                       [(fW2[e].rearrange("(k p) d -> p k d", p=P), KH) for e in range(E)]

            def load_x(b, s):
                act.dma_start(xw[s][:], x_step[STEPS - 1 - b]).then_inc(x_dma[s], 16)

            def norm_x(b, s, p):
                if p == 0:
                    act.wait_ge(x_dma[s], 16)
                    act.sem_inc(x_dma[s], -16)
                act.wait_ge(hw_free, 1)
                act.sem_inc(hw_free, -1)
                for i in (2 * p, 2 * p + 1):
                    a = bass.ds(STEPS - 1 - b, 1)
                    ins = act.activation(hw[:, i, :], xw[s][:, i, :], ACT.Identity, bias=shift_step[:, i, a],
                                         scale=rstd_step[:, i, a])
                ins.then_inc(hw_ready, 1)

            def copy_zT(bank, free):
                act.wait_ge(to_act, 1)
                act.sem_inc(to_act, -1)
                act.activation(zT[:].rearrange("p k n -> p (k n)"), bank, ACT.Identity).then_inc(act_chain, 1)
                act.wait_ge(act_chain, 1)
                act.sem_inc(act_chain, -1)
                act.sem_inc(free, 1)
                act.sem_inc(zT_ready, 1)

            def relu_a(p, bank, free):
                act.wait_ge(to_act, 1)
                act.sem_inc(to_act, -1)
                for j in range(KD):
                    ins = act.activation(aT[p][:, j, :], bank[:, j * D:(j + 1) * D], ACT.Relu, bias=gb1s[:, j:j + 1])
                ins.then_inc(act_chain, 1)
                act.wait_ge(act_chain, 1)
                act.sem_inc(act_chain, -1)
                act.sem_inc(free, 1)
                act.sem_inc(aT_ready, 1)

            def copy_xT(p, s, bank, free):
                act.wait_ge(to_act, 1)
                act.sem_inc(to_act, -1)
                cols = slice(2 * p * P, 2 * (p + 1) * P)
                for k in range(KD):
                    for dst in (xT32[:, k, cols], xThi[s][:, k, cols]):
                        ins = act.activation(dst, bank[:, k * D:(k + 1) * D], ACT.Identity, bias=fbs[:, k:k + 1],
                                             scale=fgs[:, k:k + 1])
                ins.then_inc(act_chain, 1)
                act.wait_ge(act_chain, 1)
                act.sem_inc(act_chain, -1)
                act.sem_inc(free, 1)
                act.sem_inc(xT_for_dve, 1)
                act.sem_inc(xT_for_pe, 1)

            def apply(dst, v, ready):
                act.wait_ge(dev_ready, 1)
                act.sem_inc(dev_ready, -1)
                for i in range(WPS):
                    ins = act.activation(dst[:, i, :], v[:, i, :], ACT.Identity, bias=small[:, 4, i:i + 1],
                                         scale=small[:, 3, i:i + 1])
                ins.then_inc(ready, 1)

            def gate_tanh():
                act.wait_ge(gap_ready, 1)
                act.sem_inc(gap_ready, -1)
                act.activation(tanh[:], gap[:], ACT.Tanh, scale=0.5).then_inc(tanh_ready, 1)

            def gelu(e, c):
                if c == 0:
                    act.wait_ge(hid_free, 1)
                    act.sem_inc(hid_free, -1)
                act.wait_ge(f1_ready, 1)
                act.sem_inc(f1_ready, -1)
                act.wait_ge(g_free, 1)
                act.sem_inc(g_free, -1)
                for dst in (g32[:, c, :], hid_hi[e % 2][:, c, :]):
                    ins = act.activation(dst, f1(c), ACT.Gelu, bias=fb1s[:, e * KH + c:e * KH + c + 1],
                                         scale=1.0 / WSCALE)
                ins.then_inc(act_chain, 1)
                act.wait_ge(act_chain, 1)
                act.sem_inc(act_chain, -1)
                act.sem_inc(f1_free, 1)
                act.sem_inc(g_ready, 1)

            def store_y(b, s):
                act.wait_ge(y_done, 1)
                act.sem_inc(y_done, -1)
                act.dma_start(out_step[STEPS - 1 - b], y[s][:]).then_inc(out_dma[s], 16)

            def y_is_free(s):
                act.wait_ge(out_dma[s], 16)
                act.sem_inc(out_dma[s], -16)
                act.sem_inc(y_free, 1)

            def first_step():
                for s in range(2):
                    act.dma_start(prime[:, s, :], x[0:1, 0:16]).then_inc(out_dma[s], 16)
                load_x(0, 0)
                load_x(1, 1)
                act.sem_inc(hw_free, 2)
                act.sem_inc(f1_free, 2)
                norm_x(0, 0, 0)
                norm_x(0, 0, 1)
                for n, (source, kk) in enumerate(w_pieces):
                    stage = g32[:, 2 * (n % 2):2 * (n % 2) + 2, :].rearrange("p a n -> p (a n)")
                    if n >= 2:
                        act.wait_ge(stage_free, 1)
                        act.sem_inc(stage_free, -1)
                    act.dma_start(stage.rearrange("p (k h) -> p k h", k=kk), source).then_inc(w_dma[n % 2], 16)
                    if n >= 1:
                        weight_hi(n - 1)
                weight_hi(len(w_pieces) - 1)
                act.wait_ge(stage_free, 2)
                act.sem_inc(stage_free, -2)
                act.sem_inc(g_free, 4)
                copy_zT(mA, mA_free)
                relu_a(0, mA, mA_free)
                copy_zT(mB, mB_free)
                relu_a(1, mB, mB_free)
                norm_x(1, 1, 0)
                y_is_free(0)
                apply(t, r, applied)
                apply(t, y[0], applied)
                apply(r, t, xn_ready)
                copy_xT(0, 0, mA, mA_free)
                copy_xT(1, 0, mB, mB_free)

            def weight_hi(n):
                stage = g32[:, 2 * (n % 2):2 * (n % 2) + 2, :].rearrange("p a n -> p (a n)")
                dst = (w1hi if n < E else w2hi)[:, n % E, :, :].rearrange("p k h -> p (k h)")
                act.wait_ge(w_dma[n % 2], 16)
                act.sem_inc(w_dma[n % 2], -16)
                act.activation(dst, stage, ACT.Copy, scale=WSCALE).then_inc(w_hi, 1)

            def body(b, s, last):
                for e in range(E + 1):
                    for c in range(KH):
                        if e < E:
                            gelu(e, c)
                        if (e, c) == (0, 0):
                            if not last:
                                act.wait_ge(xw_free, 1)
                                act.sem_inc(xw_free, -1)
                                load_x(b + 1, s)
                            norm_x(b, 1 - s, 1)
                        if (e, c) == (0, 1):
                            gate_tanh()
                        if (e, c) == (1, 0):
                            copy_zT(mA, mA_free)
                        if (e, c) == (1, 1):
                            relu_a(0, mA, mA_free)
                        if (e, c) == (2, 0):
                            copy_zT(mB, mB_free)
                        if (e, c) == (2, 1):
                            relu_a(1, mB, mB_free)
                        if (e, c) == (2, 3):
                            y_is_free(1 - s)
                        if (e, c) == (3, 1) and not last:
                            norm_x(b + 1, s, 0)
                        if (e, c) == (4, 0):
                            apply(t, r, applied)
                        if (e, c) == (5, 3):
                            apply(t, y[1 - s], applied)
                        if (e, c) == (6, 3):
                            apply(r, t, xn_ready)
                        if (e, c) == (7, 1):
                            copy_xT(0, 1 - s, mA, mA_free)
                        if (e, c) == (7, 2):
                            copy_xT(1, 1 - s, mB, mB_free)
                store_y(b - 1, s)

            def ffn_only():
                s = (STEPS - 1) % 2
                for e in range(E):
                    for c in range(KH):
                        gelu(e, c)
                        if (e, c) == (0, 1):
                            gate_tanh()
                store_y(STEPS - 1, s)
                for s in range(2):
                    act.wait_ge(out_dma[s], 16)

            steps(act, first_step, body, ffn_only)

        @block.vector
        def _(dve):
            place, tile = dve.alloc_register("place"), dve.alloc_register("tile")
            dve.reg_mov(place, 0)

            def onehots(k, half):
                dve.reg_load(tile, lo_row[0:1, bass.ds(k, 1)])
                nb = dve.value_load(nb_row[0:1, bass.ds(k, 1)], min_val=1, max_val=1 << 20)
                dve.tensor_scalar(iota_k[:, half, :], iota16[:], base[:, bass.ds(k, 1)], None, ALU.add).then_inc(chain, 1)
                dve.wait_ge(chain, 1)
                dve.sem_inc(chain, -1)
                with dve.Fori(0, nb):
                    dve.wait_ge(onehot_free, 1)
                    dve.sem_inc(onehot_free, -1)
                    to = dve.snap(place, min_val=0, max_val=(G - 1) * U * P)
                    at = dve.snap(tile, min_val=0, max_val=TCOLS - U)
                    dve.tensor_tensor(onehot[:, bass.ds(to, U * P)].rearrange("p (t e) -> p t e", t=U),
                                      iota_k[:, half, :].unsqueeze(1).broadcast_to([P, U, P]),
                                      dst_f[:, bass.ds(at, U)].unsqueeze(2).broadcast_to([P, U, P]),
                                      ALU.is_equal).then_inc(onehot_ready, 1)
                    dve.reg_add(place, place, U * P)
                    dve.reg_alu(place, place, G * U * P - 1, ALU.bitwise_and)
                    dve.reg_add(tile, tile, U)

            def add_z(i):
                if i % 2 == 0:
                    dve.wait_ge(hw_ready, 1)
                    dve.sem_inc(hw_ready, -1)
                    dve.wait_ge(z_free, 1)
                    dve.sem_inc(z_free, -1)
                dve.wait_ge(agg_ready, 1)
                dve.sem_inc(agg_ready, -1)
                dve.scalar_tensor_tensor(out=z[:, i, :], in0=hw[:, i, :], scalar=opeps[:, 0:1],
                                         in1=agg(i % 2)[:, 0:D], op0=ALU.mult, op1=ALU.add).then_inc(chain, 1)
                dve.wait_ge(chain, 1)
                dve.sem_inc(chain, -1)
                dve.tensor_tensor(z[:, i, :], z[:, i, :], agg(i % 2)[:, D:2 * D], ALU.add).then_inc(z_ready, 1)

            def residual(p, bank, free):
                two = slice(2 * p, 2 * p + 2)
                dve.tensor_tensor(r[:, two, :], hw[:, two, :], gb2s[:].unsqueeze(1).broadcast_to([P, 2, D]),
                                  ALU.add).then_inc(chain, 1)
                dve.wait_ge(chain, 1)
                dve.sem_inc(chain, -1)
                dve.sem_inc(hw_free, 1)
                dve.wait_ge(to_dve, 1)
                dve.sem_inc(to_dve, -1)
                dve.tensor_tensor(r[:, two, :], r[:, two, :], bank.rearrange("p (i d) -> p i d", i=2),
                                  ALU.add).then_inc(chain, 1)
                dve.wait_ge(chain, 1)
                dve.sem_inc(chain, -1)
                dve.sem_inc(free, 1)

            rstd, shift = small[:, 3, 0:WPS], small[:, 4, 0:WPS]

            def moments(v):
                for i in range(WPS):
                    ins = dve.bn_stats(bstats[:, i, :], v[:, i, :])
                ins.then_inc(chain, 1)
                dve.wait_ge(chain, 1)
                dve.sem_inc(chain, -1)
                for i in range(WPS):
                    ins = dve.bn_aggr(bmv[:, i, :], bstats[:, i, :])
                ins.then_inc(chain, 1)
                dve.wait_ge(chain, 1)
                dve.sem_inc(chain, -1)

            def deviations():
                rsqrt(dve, chain, rstd, bmv[:, :, 1], [small[:, n, 0:WPS] for n in range(3)])
                dve.scalar_tensor_tensor(out=shift, in0=bmv[:, :, 0], scalar=-1.0, in1=rstd,
                                         op0=ALU.mult, op1=ALU.mult).then_inc(dev_ready, 1)

            def over_i(a):
                return a.unsqueeze(1).broadcast_to([P, WPS, D])

            def ln_gamma():
                dve.wait_ge(applied, 1)
                dve.sem_inc(applied, -1)
                dve.tensor_tensor(t[:], t[:], over_i(ggs[:]), ALU.mult).then_inc(chain, 1)
                dve.wait_ge(chain, 1)
                dve.sem_inc(chain, -1)

            def ln_beta():
                dve.tensor_tensor(t[:], t[:], over_i(gbs[:]), ALU.add).then_inc(chain, 1)
                dve.wait_ge(chain, 1)
                dve.sem_inc(chain, -1)

            def add_x(s):
                dve.wait_ge(y_free, 1)
                dve.sem_inc(y_free, -1)
                dve.scalar_tensor_tensor(out=y[s][:], in0=t[:], scalar=0.0, in1=xw[s][:], op0=ALU.max,
                                         op1=ALU.add).then_inc(chain, 1)
                dve.wait_ge(chain, 1)
                dve.sem_inc(chain, -1)
                dve.sem_inc(xw_free, 1)

            def second_moments():
                dve.wait_ge(applied, 1)
                dve.sem_inc(applied, -1)
                moments(t)

            def split_xT(p, s):
                dve.wait_ge(xT_for_dve, 1)
                dve.sem_inc(xT_for_dve, -1)
                cols = slice(2 * p * P, 2 * (p + 1) * P)
                dve.tensor_tensor(xTlo[s][:, :, cols], xT32[:, :, cols], xThi[s][:, :, cols], ALU.subtract)\
                   .then_inc(xlo_ready, 1)

            def top_two():
                dve.wait_ge(to_dve, 1)
                dve.sem_inc(to_dve, -1)
                dve.tensor_tensor(logit[:], mA[:, 0:WPS * E].rearrange("p (i e) -> p i e", i=WPS),
                                  fbrs[:].unsqueeze(1).broadcast_to([P, WPS, E]), ALU.add).then_inc(chain, 1)
                dve.wait_ge(chain, 1)
                dve.sem_inc(chain, -1)
                dve.sem_inc(mA_free, 1)
                for i in range(WPS):
                    ins = dve.max(top[:, i, :], logit[:, i, :])
                ins.then_inc(chain, 1)
                dve.wait_ge(chain, 1)
                dve.sem_inc(chain, -1)
                dve.tensor_tensor(gap[:], top[:, :, 0], top[:, :, 1], ALU.subtract).then_inc(gap_ready, 1)
                for i in range(WPS):
                    ins = dve.max_index(top_i[:, i, :], top[:, i, :], logit[:, i, :])
                ins.then_inc(chain, 1)
                dve.wait_ge(chain, 1)
                dve.sem_inc(chain, -1)
                dve.tensor_copy(top_f[:], top_i[:]).then_inc(chain, 1)
                dve.wait_ge(chain, 1)
                dve.sem_inc(chain, -1)

            def gates(s):
                dve.wait_ge(tanh_ready, 1)
                dve.sem_inc(tanh_ready, -1)
                half = 0.5 / WSCALE
                dve.tensor_scalar(wtop[:, 0, :], tanh[:], half, half, ALU.mult, ALU.add)
                dve.tensor_scalar(wtop[:, 1, :], tanh[:], -half, half, ALU.mult, ALU.add).then_inc(chain, 1)
                dve.wait_ge(chain, 1)
                dve.sem_inc(chain, -1)
                for n, dst in enumerate((wf[s], wsel)):
                    for i in range(WPS):
                        ins = dve.tensor_scalar(dst[:, i, :], iota8[:], top_f[:, i, n:n + 1], wtop[:, n, i:i + 1],
                                                ALU.is_equal, ALU.mult)
                ins.then_inc(chain, 1)
                dve.wait_ge(chain, 1)
                dve.sem_inc(chain, -1)
                dve.tensor_tensor(wf[s][:], wf[s][:], wsel[:], ALU.add).then_inc(chain, 1)
                dve.wait_ge(chain, 1)
                dve.sem_inc(chain, -1)
                dve.sem_inc(wf_ready, 1)

            def copy_wfT():
                dve.wait_ge(to_dve, 1)
                dve.sem_inc(to_dve, -1)
                dve.tensor_copy(wfT, mB[0:E, :]).then_inc(chain, 1)
                dve.wait_ge(chain, 1)
                dve.sem_inc(chain, -1)
                dve.sem_inc(mB_free, 1)
                dve.sem_inc(wfT_ready, 1)

            def start_y(p, s, bank, free):
                dve.wait_ge(to_dve, 1)
                dve.sem_inc(to_dve, -1)
                two = slice(2 * p, 2 * p + 2)
                dve.tensor_tensor(y[s][:, two, :], y[s][:, two, :], bank.rearrange("p (i d) -> p i d", i=2),
                                  ALU.add).then_inc(chain, 1)
                dve.wait_ge(chain, 1)
                dve.sem_inc(chain, -1)
                dve.sem_inc(free, 1)

            def rest_of_gelu(e, c):
                dve.wait_ge(g_ready, 1)
                dve.sem_inc(g_ready, -1)
                dve.tensor_tensor(hid_lo[e % 2][:, c, :], g32[:, c, :], hid_hi[e % 2][:, c, :],
                                  ALU.subtract).then_inc(lo_ready, 1)

            def add_y(e, tb, s):
                dve.wait_ge(f2_ready, 1)
                dve.sem_inc(f2_ready, -1)
                if tb == WPS - 1:
                    dve.sem_inc(hid_free, 1)
                ins = dve.scalar_tensor_tensor(out=y[s][:, tb, :], in0=f2(tb), scalar=wf[s][:, tb, e:e + 1],
                                               in1=y[s][:, tb, :], op0=ALU.mult, op1=ALU.add)
                if (e, tb) == (E - 1, WPS - 1):
                    ins.then_inc(chain, 1)
                    dve.wait_ge(chain, 1)
                    dve.sem_inc(chain, -1)
                    dve.sem_inc(f2_free, 1)
                    dve.sem_inc(y_done, 1)
                else:
                    ins.then_inc(f2_free, 1)

            def first_step():
                dve.sem_inc(z_free, 2)
                dve.sem_inc(f2_free, 2)
                dve.sem_inc(hid_free, 2)
                dve.tensor_scalar(b2s[:], fb2s[:], WSCALE, None, ALU.mult)
                dve.tensor_scalar(opeps[:], eps1[:], 1.0, None, ALU.add).then_inc(chain, 1)
                dve.wait_ge(chain, 1)
                dve.sem_inc(chain, -1)
                dve.sem_inc(opeps_ready, 1)
                onehots(0, 0)
                onehots(1, 1)
                add_z(0)
                for n in range(2 * E):
                    stage = g32[:, 2 * (n % 2):2 * (n % 2) + 2, :].rearrange("p a n -> p (a n)")
                    hi, lo = ((w1hi, w1lo) if n < E else (w2hi, w2lo))
                    dve.wait_ge(w_hi, 1)
                    dve.sem_inc(w_hi, -1)
                    dve.scalar_tensor_tensor(out=lo[:, n % E].rearrange("p k h -> p (k h)"), in0=stage, scalar=WSCALE,
                                             in1=hi[:, n % E].rearrange("p k h -> p (k h)"), op0=ALU.mult,
                                             op1=ALU.subtract).then_inc(stage_free, 1)
                onehots(2, 0)
                add_z(1)
                onehots(3, 1)
                add_z(2)
                residual(0, mA, mA_free)
                add_z(3)
                residual(1, mB, mB_free)
                onehots(4, 0)
                onehots(5, 1)
                moments(r)
                deviations()
                ln_gamma()
                ln_beta()
                add_x(0)
                moments(y[0])
                deviations()
                second_moments()
                deviations()
                add_z(0)
                add_z(1)
                split_xT(0, 0)
                split_xT(1, 0)

            def body(b, s, last):
                for e in range(E + 1):
                    for c in range(KH):
                        if (e, c) == (0, 0):
                            onehots(4 * b + 2, 0)
                        if e < E:
                            rest_of_gelu(e, c)
                        if e > 0:
                            add_y(e - 1, c, s)
                        if (e, c) == (0, 0):
                            top_two()
                        if (e, c) == (0, 1):
                            gates(s)
                        if (e, c) == (0, 2):
                            copy_wfT()
                        if (e, c) == (0, 3):
                            start_y(0, s, mA, mA_free)
                            start_y(1, s, mB, mB_free)
                        if (e, c) == (1, 0):
                            add_z(2)
                        if (e, c) == (1, 1):
                            onehots(4 * b + 3, 1)
                        if (e, c) == (1, 3):
                            add_z(3)
                        if (e, c) == (2, 0):
                            residual(0, mA, mA_free)
                        if (e, c) == (3, 0):
                            residual(1, mB, mB_free)
                        if (e, c) == (3, 1):
                            moments(r)
                        if (e, c) == (3, 2):
                            deviations()
                        if (e, c) == (3, 3) and not last:
                            onehots(4 * b + 4, 0)
                        if (e, c) == (4, 1):
                            ln_gamma()
                        if (e, c) == (4, 2):
                            ln_beta()
                        if (e, c) == (4, 3):
                            add_x(1 - s)
                        if (e, c) == (5, 0):
                            moments(y[1 - s])
                        if (e, c) == (5, 1):
                            deviations()
                        if (e, c) == (5, 2) and not last:
                            add_z(0)
                        if (e, c) == (5, 3) and not last:
                            onehots(4 * b + 5, 1)
                        if (e, c) == (6, 0):
                            second_moments()
                        if (e, c) == (6, 1):
                            deviations()
                        if (e, c) == (7, 0) and not last:
                            add_z(1)
                        if (e, c) == (7, 2):
                            split_xT(0, 1 - s)
                        if (e, c) == (7, 3):
                            split_xT(1, 1 - s)

            def ffn_only():
                dve.sem_inc(onehot_ready, G)
                s = (STEPS - 1) % 2
                for e in range(E + 1):
                    for c in range(KH):
                        if e < E:
                            rest_of_gelu(e, c)
                        if e > 0:
                            add_y(e - 1, c, s)
                        if (e, c) == (0, 0):
                            top_two()
                        if (e, c) == (0, 1):
                            gates(s)
                        if (e, c) == (0, 2):
                            copy_wfT()
                        if (e, c) == (0, 3):
                            start_y(0, s, mA, mA_free)
                            start_y(1, s, mB, mB_free)

            steps(dve, first_step, body, ffn_only)


def kernel(**inputs):
    import numpy as np
    import concourse.bacc as bacc
    from concourse.bass_utils import run_bass_kernel_spmd

    nodes = inputs["x"].shape[0]
    x = np.zeros((ROWS, D), np.float32)
    x[:nodes] = inputs["x"]
    src = np.zeros(TPAD * P, np.int32)
    src[:EDGES] = inputs["src"]
    dst = np.full(TPAD * P, NOWHERE, np.int32)
    dst[:EDGES] = inputs["dst"]
    arrays = {
        "x": x,
        "src_cols": np.ascontiguousarray(src.reshape(TPAD, P)[:TCOLS].T),
        "dst_cols": np.ascontiguousarray(dst.reshape(TPAD, P)[:TCOLS].T),
        "dst_rows": dst.reshape(TPAD, P),
    }
    for name in ("gnn_W1", "gnn_b1", "gnn_W2", "gnn_b2", "gnn_eps", "gnn_gamma", "gnn_beta", "ffn_gamma", "ffn_beta",
                 "ffn_Wr", "ffn_br", "ffn_W1", "ffn_b1", "ffn_W2", "ffn_b2"):
        a = np.ascontiguousarray(inputs["L0_" + name])
        arrays[name] = a.reshape(1) if a.ndim == 0 else a
    nc = bacc.Bacc("TRN2", target_bir_lowering=False, num_devices=1)
    args = [nc.dram_tensor("in_" + n, a.shape, mybir.dt.from_np(a.dtype), kind="ExternalInput").ap()
            for n, a in arrays.items()]
    out = nc.dram_tensor("out", (ROWS, D), F32, kind="ExternalOutput").ap()
    gnn_moe_kernel(nc, *args, out)
    r = run_bass_kernel_spmd(nc, [{"in_" + n: a for n, a in arrays.items()}], core_ids=[0])
    return r.results[0]["out"][:nodes]
```

```python
from contextlib import ExitStack

import concourse.bass as bass
from concourse import mybir

F32, F16, I32, U32 = mybir.dt.float32, mybir.dt.float16, mybir.dt.int32, mybir.dt.uint32
ACT, ALU = mybir.ActivationFunctionType, mybir.AluOpType
AX_X = mybir.AxisListType.X

P = 128
D, KD = 256, 2
H, KH, E = 512, 4, 8
WPS = 4
STEPS = 25
WINDOWS = WPS * STEPS
ROWS = WINDOWS * P
EDGES = 200000
TILES = -(-EDGES // P)
TC = 13
TPAD = TC * P

NOWHERE = ROWS
U = 6
DIV_BITS = 12
DIV_MUL = (1 << DIV_BITS) // U + 1
assert all(n * DIV_MUL >> DIV_BITS == n // U for n in range(TILES + U + 1))
G = 4
TCOLS = TILES + U + 1
EPS = 1e-5
WSCALE = 64.0
CH = 10
CHUNKS = WINDOWS // CH
XB = 4
ZN = 8
LAG = 5
NE = E * KH
PARTS = ((12, 2), (14, 1), (16, 1), (18, 1), (20, 1), (22, 1), (25, 1), (28, None))
RSQRT_SEED = float(0x5F3759DF)


def rsqrt_seed(dve, chain, y, var, tmp):
    ve, hv, a = tmp
    dve.tensor_scalar(ve, var, EPS, None, ALU.add).then_inc(chain, 1)
    dve.wait_ge(chain, 1)
    dve.sem_inc(chain, -1)
    dve.tensor_scalar(hv, ve, -0.5, None, ALU.mult)
    dve.tensor_scalar(a.bitcast(I32), ve.bitcast(I32), 1, None, ALU.logical_shift_right).then_inc(chain, 1)
    dve.wait_ge(chain, 1)
    dve.sem_inc(chain, -1)
    dve.tensor_scalar(y.bitcast(I32), a.bitcast(I32), -1.0, RSQRT_SEED, ALU.mult, ALU.add).then_inc(chain, 1)
    dve.wait_ge(chain, 1)
    dve.sem_inc(chain, -1)
    newton(dve, chain, y, tmp)


def newton(dve, chain, y, tmp):
    _, hv, a = tmp
    dve.tensor_tensor(a, y, y, ALU.mult).then_inc(chain, 1)
    dve.wait_ge(chain, 1)
    dve.sem_inc(chain, -1)
    dve.tensor_tensor(a, a, hv, ALU.mult).then_inc(chain, 1)
    dve.wait_ge(chain, 1)
    dve.sem_inc(chain, -1)
    dve.scalar_tensor_tensor(out=y, in0=a, scalar=1.5, in1=y, op0=ALU.add, op1=ALU.mult).then_inc(chain, 1)
    dve.wait_ge(chain, 1)
    dve.sem_inc(chain, -1)


def gnn_moe_kernel(nc, x, src_cols, dst_cols, dst_rows, gW1, gb1, gW2, gb2, geps, ggamma, gbeta,
                   fgamma, fbeta, fWr, fbr, fW1, fb1, fW2, fb2, out):
    table = nc.dram_tensor("normed_rows", (ROWS, 2 * D), F16, kind="Internal").ap()
    with ExitStack() as ctx:
        def sb(name, shape, dt=F32):
            return ctx.enter_context(nc.sbuf_tensor(name, shape, dt))

        def sem(name):
            return ctx.enter_context(nc.semaphore(name))

        psum = ctx.enter_context(nc.psum_tensor("psum", [P, 8, 512], F32))
        src_idx = sb("src_idx", [P, TCOLS], I32)
        dst_f = sb("dst_f", [P, TCOLS])
        rstd0 = sb("rstd0", [P, WINDOWS])
        shift0 = sb("shift0", [P, WINDOWS])
        lo_row = sb("lo_row", [1, 128], I32)
        nb_row = sb("nb_row", [1, 128], I32)
        rounds = sb("rounds", [1, 8], I32)
        base = sb("base", [P, WINDOWS])
        ident = sb("ident", [P, P])
        iota16 = sb("iota16", [P, P], F16)
        iota8 = sb("iota8", [P, 8])
        zeros16 = sb("zeros16", [P, 512], F16)
        gW1s, gW2s = sb("gW1s", [P, KD, D]), sb("gW2s", [P, KD, D])
        gb1s = sb("gb1s", [P, KD])
        gb2s, ggs, gbs = sb("gb2s", [P, D]), sb("ggs", [P, D]), sb("gbs", [P, D])
        eps1 = sb("eps1", [P, 1])
        fgs, fbs = sb("fgs", [P, KD]), sb("fbs", [P, KD])
        fWrs, fbrs = sb("fWrs", [P, KD, E]), sb("fbrs", [P, E])
        fb1s = sb("fb1s", [P, E * KH])
        fb2s = sb("fb2s", [E, D])
        small = sb("small", [P, 5, 2 * CH])
        iota_k = sb("iota_k", [P, 2, P])

        chain = sem("chain")
        const_in = sem("const_in")
        edges_in = sem("edges_in")

        with ExitStack() as first:
            def fsb(name, shape, dt=F32):
                return first.enter_context(nc.sbuf_tensor(name, shape, dt))

            xin = [fsb(f"xin{u}", [P, CH, D]) for u in range(XB)]
            h32 = [fsb(f"h32_{s}", [P, CH, D]) for s in range(2)]
            pair = [fsb(f"pair{s}", [P, CH, 2 * D], F16) for s in range(2)]
            stats = fsb("stats", [P, 2 * CH, 6])
            mv = fsb("mv", [P, 2 * CH, 2])
            dst_i = fsb("dst_i", [P, TCOLS], I32)
            rows_i = fsb("rows_i", [P, TC, P], I32)
            tmin, tmax = fsb("tmin", [P, TC]), fsb("tmax", [P, TC])
            base_end = fsb("base_end", [P, WINDOWS])
            tnum_i = fsb("tnum_i", [P, TC], I32)
            tnum = fsb("tnum", [P, 2, TC])
            base_i = fsb("base_i", [P, WINDOWS], I32)
            iota_i = fsb("iota_i", [P, P], I32)
            m1 = fsb("m1", [P, TC, WINDOWS])
            m2 = fsb("m2", [P, TC, WINDOWS])
            ends = fsb("ends", [P, 2, WINDOWS])
            ends_k = fsb("ends_k", [P, 2])
            lo_k, nt_k = fsb("lo_k", [P, 1]), fsb("nt_k", [P, 1])
            row_f = fsb("row_f", [1, 2, WINDOWS])
            total = fsb("total", [1, 1])
            prime0 = fsb("prime0", [1, 2, 16])

            x_in = [first.enter_context(nc.semaphore(f"x_in{u}")) for u in range(XB)]
            pair_out = [first.enter_context(nc.semaphore(f"pair_out{s}")) for s in range(2)]
            x_free, stats_ready, high_ready, pair_ready = (
                first.enter_context(nc.semaphore(n)) for n in ("x_free", "stats_ready", "high_ready", "pair_ready"))
            h_free, pool_const, pool_chain = (
                first.enter_context(nc.semaphore(n)) for n in ("h_free", "pool_const", "pool_chain"))
            ends_ready, ends_turned, cols_ready, cols_turned = (
                first.enter_context(nc.semaphore(n)) for n in ("ends_ready", "ends_turned", "cols_ready", "cols_turned"))
            ident_ready = first.enter_context(nc.semaphore("ident_ready"))
            act_chain = first.enter_context(nc.semaphore("act_chain0"))
            block = first.enter_context(nc.Block())
            x_chunk = x.rearrange("(c i p) d -> c p i d", i=CH, p=P)
            table_chunk = table.rearrange("(c i p) d -> c p i d", i=CH, p=P)

            @block.sync
            def _(sp):
                for u in range(XB):
                    sp.dma_start(xin[u][:], x_chunk[u]).then_inc(x_in[u], 16)
                for dst, source in ((rows_i[:], dst_rows.rearrange("(c p) e -> p c e", p=P)), (dst_i[:], dst_cols),
                                    (src_idx[:], src_cols)):
                    sp.dma_start(dst, source).then_inc(edges_in, 16)
                for c in range(CHUNKS):
                    if c + XB < CHUNKS:
                        sp.wait_ge(x_free, 1)
                        sp.sem_inc(x_free, -1)
                        sp.dma_start(xin[c % XB][:], x_chunk[c + XB]).then_inc(x_in[c % XB], 16)
                    sp.wait_ge(pair_ready, 1)
                    sp.sem_inc(pair_ready, -1)
                    sp.dma_start(table_chunk[c], pair[c % 2][:]).then_inc(pair_out[c % 2], 16)

            def over_chunks(eng, turn):
                with eng.Fori(0, CHUNKS // XB) as j:
                    for u in range(0, XB, 2):
                        turn(XB * j + u, u)
                turn(CHUNKS - 2, 0)

            @block.gpsimd
            def _(pool):
                pool.memset(ident[:], 0.0).then_inc(pool_chain, 1)
                pool.wait_ge(pool_chain, 1)
                pool.sem_inc(pool_chain, -1)
                pool.affine_select(out=ident[:], in_=ident[:], compare_op=ALU.not_equal, fill=1.0, base=0,
                                   pattern=[[-1, P]], channel_multiplier=1).then_inc(ident_ready, 1)
                pool.iota(tnum_i[:], pattern=[[P, TC]], base=0, channel_multiplier=1)
                pool.iota(base_i[:], pattern=[[-P, STEPS], [STEPS * P, WPS]], base=(STEPS - 1) * P,
                          channel_multiplier=0)
                pool.iota(iota_i[:], pattern=[[1, P]], base=0, channel_multiplier=0)
                pool.memset(zeros16[:], 0.0)
                pool.memset(lo_row[:], 0)
                pool.memset(nb_row[:], 1 << 20).then_inc(pool_const, 1)

                def rests(c0, u):
                    for s in range(2):
                        pool.wait_ge(high_ready, 1)
                        pool.sem_inc(high_ready, -1)
                        pool.tensor_tensor(pair[s][:, :, D:2 * D], h32[s][:], pair[s][:, :, 0:D], ALU.subtract)\
                            .then_inc(pool_chain, 1)
                        pool.wait_ge(pool_chain, 1)
                        pool.sem_inc(pool_chain, -1)
                        pool.sem_inc(pair_ready, 1)
                        pool.sem_inc(h_free, 1)

                over_chunks(pool, rests)

            @block.scalar
            def _(act):
                with nc.allow_non_contiguous_dma(reason="small constants, once"):
                    loads = [
                        (gW1s[:], gW1.rearrange("(k p) n -> p k n", p=P)), (gW2s[:], gW2.rearrange("(k p) n -> p k n", p=P)),
                        (gb1s[:], gb1.rearrange("(k p) -> p k", p=P)),
                        (gb2s[:], gb2.partition_broadcast(P)), (ggs[:], ggamma.partition_broadcast(P)),
                        (gbs[:], gbeta.partition_broadcast(P)), (eps1[:], geps.partition_broadcast(P)),
                        (fgs[:], fgamma.rearrange("(k p) -> p k", p=P)), (fbs[:], fbeta.rearrange("(k p) -> p k", p=P)),
                        (fWrs[:], fWr.rearrange("(k p) e -> p k e", p=P)), (fbrs[:], fbr.partition_broadcast(P)),
                        (fb1s[:], fb1.rearrange("e (j p) -> p (e j)", p=P)), (fb2s[:], fb2),
                    ]
                    for dst, source in loads:
                        act.dma_start(dst, source).then_inc(const_in, 16)

                def norm(c0, u):
                    act.wait_ge(stats_ready, 1)
                    act.sem_inc(stats_ready, -1)
                    for s in range(2):
                        act.wait_ge(h_free, 1)
                        act.sem_inc(h_free, -1)
                        for i in range(CH):
                            w = (c0 + s) * CH + i
                            ins = act.activation(h32[s][:, i, :], xin[u + s][:, i, :], ACT.Identity,
                                                 bias=shift0[:, bass.ds(w, 1)], scale=rstd0[:, bass.ds(w, 1)])
                        ins.then_inc(act_chain, 1)
                        act.wait_ge(act_chain, 1)
                        act.sem_inc(act_chain, -1)
                        act.sem_inc(x_free, 1)
                        act.wait_ge(pair_out[s], 16)
                        act.sem_inc(pair_out[s], -16)
                        act.activation(pair[s][:, :, 0:D], h32[s][:], ACT.Identity).then_inc(act_chain, 1)
                        act.wait_ge(act_chain, 1)
                        act.sem_inc(act_chain, -1)
                        act.sem_inc(high_ready, 1)

                act.sem_inc(h_free, 2)
                for s in range(2):
                    act.dma_start(prime0[:, s, :], x[0:1, 0:16]).then_inc(pair_out[s], 16)
                over_chunks(act, norm)
                for s in range(2):
                    act.wait_ge(pair_out[s], 16)
                    act.sem_inc(pair_out[s], -16)
                act.wait_ge(const_in, 16 * len(loads))

            @block.vector
            def _(dve):
                def moments(c0, u):
                    for s in range(2):
                        dve.wait_ge(x_in[u + s], 16)
                        dve.sem_inc(x_in[u + s], -16)
                        for i in range(CH):
                            ins = dve.bn_stats(stats[:, s * CH + i, :], xin[u + s][:, i, :])
                    ins.then_inc(chain, 1)
                    dve.wait_ge(chain, 1)
                    dve.sem_inc(chain, -1)
                    for i in range(2 * CH):
                        ins = dve.bn_aggr(mv[:, i, :], stats[:, i, :])
                    ins.then_inc(chain, 1)
                    dve.wait_ge(chain, 1)
                    dve.sem_inc(chain, -1)
                    col = bass.ds(c0 * CH, 2 * CH)
                    tmp = [small[:, n, :] for n in range(3)]
                    rsqrt_seed(dve, chain, small[:, 3, :], mv[:, :, 1], tmp)
                    newton(dve, chain, small[:, 3, :], tmp)
                    newton(dve, chain, small[:, 3, :], tmp)
                    dve.tensor_copy(rstd0[:, col], small[:, 3, :])
                    dve.scalar_tensor_tensor(out=shift0[:, col], in0=mv[:, :, 0], scalar=-1.0,
                                             in1=small[:, 3, :], op0=ALU.mult, op1=ALU.mult).then_inc(chain, 1)
                    dve.wait_ge(chain, 1)
                    dve.sem_inc(chain, -1)
                    dve.sem_inc(stats_ready, 1)

                over_chunks(dve, moments)

                dve.wait_ge(pool_const, 1)
                dve.sem_inc(pool_const, -1)
                dve.wait_ge(edges_in, 48)
                dve.tensor_copy(dst_f[:], dst_i[:])
                dve.tensor_copy(base[:], base_i[:])
                dve.tensor_scalar(base_end[:], base_i[:], float(P - 1), None, ALU.add)
                dve.tensor_copy(iota16[:], iota_i[:])
                dve.tensor_copy(iota8[:], iota_i[:, 0:8])
                dve.tensor_scalar(tnum[:, 0, :], tnum_i[:], 1.0, None, ALU.add)
                dve.tensor_scalar(tnum[:, 1, :], tnum_i[:], -1.0, float(TILES), ALU.mult, ALU.add)
                dve.tensor_reduce(tmin[:], rows_i[:], AX_X, ALU.min)
                dve.tensor_reduce(tmax[:], rows_i[:], AX_X, ALU.max).then_inc(chain, 1)
                dve.wait_ge(chain, 1)
                dve.sem_inc(chain, -1)

                def over_k(a):
                    return a.unsqueeze(2).broadcast_to([P, TC, WINDOWS])

                def over_t(a):
                    return a.unsqueeze(1).broadcast_to([P, TC, WINDOWS])

                dve.tensor_tensor(m1[:], over_t(base[:]), over_k(tmax[:]), ALU.is_le)
                dve.tensor_tensor(m2[:], over_t(base_end[:]), over_k(tmin[:]), ALU.is_ge).then_inc(chain, 1)
                dve.wait_ge(chain, 1)
                dve.sem_inc(chain, -1)
                dve.tensor_tensor(m1[:], m1[:], m2[:], ALU.mult).then_inc(chain, 1)
                dve.wait_ge(chain, 1)
                dve.sem_inc(chain, -1)
                for n in range(2):
                    dve.tensor_tensor(m2[:], m1[:], over_k(tnum[:, n, :]), ALU.mult).then_inc(chain, 1)
                    dve.wait_ge(chain, 1)
                    dve.sem_inc(chain, -1)
                    dve.tensor_reduce(ends[:, n, :], m2[:].rearrange("p c k -> p k c"), AX_X, ALU.max).then_inc(chain, 1)
                    dve.wait_ge(chain, 1)
                    dve.sem_inc(chain, -1)
                dve.sem_inc(ends_ready, 1)
                dve.wait_ge(ends_turned, 1)
                dve.sem_inc(ends_turned, -1)
                turned = psum[0:WINDOWS, 0, 0:2 * P].rearrange("k (n p) -> k n p", n=2)
                dve.tensor_reduce(ends_k[0:WINDOWS, :], turned, AX_X, ALU.max).then_inc(chain, 1)
                dve.wait_ge(chain, 1)
                dve.sem_inc(chain, -1)
                dve.tensor_scalar(lo_k[0:WINDOWS, :], ends_k[0:WINDOWS, 1:2], -1.0, float(TILES),
                                  ALU.mult, ALU.add).then_inc(chain, 1)
                dve.wait_ge(chain, 1)
                dve.sem_inc(chain, -1)
                dve.tensor_scalar(lo_k[0:WINDOWS, :], lo_k[0:WINDOWS, :], float(TILES - 1), None, ALU.min).then_inc(chain, 1)
                dve.wait_ge(chain, 1)
                dve.sem_inc(chain, -1)
                dve.tensor_tensor(nt_k[0:WINDOWS, :], ends_k[0:WINDOWS, 0:1], lo_k[0:WINDOWS, :],
                                  ALU.subtract).then_inc(chain, 1)
                dve.wait_ge(chain, 1)
                dve.sem_inc(chain, -1)
                dve.tensor_scalar(nt_k[0:WINDOWS, :], nt_k[0:WINDOWS, :], 1.0, float(U - 1),
                                  ALU.max, ALU.add).then_inc(chain, 1)
                dve.wait_ge(chain, 1)
                dve.sem_inc(chain, -1)
                dve.sem_inc(cols_ready, 1)
                dve.wait_ge(cols_turned, 1)
                dve.sem_inc(cols_turned, -1)
                dve.tensor_copy(lo_row[:, 0:WINDOWS], psum[0:1, 1, 0:WINDOWS])
                dve.tensor_scalar(nb_row[:, 0:WINDOWS], psum[0:1, 1, P:P + WINDOWS], float(DIV_MUL), None,
                                  ALU.mult).then_inc(chain, 1)
                dve.wait_ge(chain, 1)
                dve.sem_inc(chain, -1)
                dve.tensor_scalar(nb_row[:, 0:WINDOWS], nb_row[:, 0:WINDOWS], DIV_BITS, None,
                                  ALU.logical_shift_right).then_inc(chain, 1)
                dve.wait_ge(chain, 1)
                dve.sem_inc(chain, -1)
                dve.tensor_copy(row_f[:, 0, :], nb_row[:, 0:WINDOWS]).then_inc(chain, 1)
                dve.wait_ge(chain, 1)
                dve.sem_inc(chain, -1)
                dve.tensor_reduce(total[:], row_f[:, 0, :], AX_X, ALU.add).then_inc(chain, 1)
                dve.wait_ge(chain, 1)
                dve.sem_inc(chain, -1)
                dve.tensor_scalar(rounds[:, 0:1], total[:], float(G - 1), None, ALU.add).then_inc(chain, 1)
                dve.wait_ge(chain, 1)
                dve.sem_inc(chain, -1)
                dve.tensor_scalar(rounds[:, 1:2], rounds[:, 0:1], G.bit_length() - 1, None,
                                  ALU.logical_shift_right).then_inc(chain, 1)
                dve.wait_ge(chain, 1)
                dve.sem_inc(chain, -1)

            @block.tensor
            def _(pe):
                pe.wait_ge(ident_ready, 1)
                pe.sem_inc(ident_ready, -1)
                pe.wait_ge(ends_ready, 1)
                pe.sem_inc(ends_ready, -1)
                for n in range(2):
                    ins = pe.transpose(psum[0:WINDOWS, 0, n * P:(n + 1) * P], ends[:, n, :], ident[:])
                ins.then_inc(ends_turned, 1)
                pe.wait_ge(cols_ready, 1)
                pe.sem_inc(cols_ready, -1)
                for n, col in enumerate((lo_k, nt_k)):
                    ins = pe.transpose(psum[0:1, 1, n * P:n * P + WINDOWS], col[0:WINDOWS, :],
                                       ident[0:WINDOWS, 0:WINDOWS])
                ins.then_inc(cols_turned, 1)

        ring = sb("ring", [P, G * U * 2 * D], F16)
        idx_now = sb("idx_now", [P, G, U], I32)
        onehot = sb("onehot", [P, G * U * P], F16)
        w1hi, w1lo = sb("w1hi", [P, E, KD, H], F16), sb("w1lo", [P, E, KD, H], F16)
        w2hi, w2lo = sb("w2hi", [P, E, KH, D], F16), sb("w2lo", [P, E, KH, D], F16)
        b2s = sb("b2s", [E, D])
        xw = [sb(f"xw{s}", [P, WPS, D]) for s in range(2)]
        hw = sb("hw", [P, WPS, D])
        z = sb("z", [P, WPS, D])
        zT = sb("zT", [P, KD, 2 * P])
        aT = [sb(f"aT{p}", [P, KD, 2 * P]) for p in range(2)]
        r = sb("r", [P, WPS, D])
        t = sb("t", [P, WPS, D])
        bstats = sb("bstats", [P, WPS, 6])
        bmv = sb("bmv", [P, WPS, 2])
        opeps = sb("opeps", [P, 1])
        xT32 = sb("xT32", [P, KD, WPS * P])
        xThi = [sb(f"xThi{s}", [P, KD, WPS * P], F16) for s in range(2)]
        xTlo = [sb(f"xTlo{s}", [P, KD, WPS * P], F16) for s in range(2)]
        logit = sb("logit", [P, WPS, E])
        top = sb("top", [P, WPS, 8])
        top_i = sb("top_i", [P, WPS, 8], U32)
        top_f = sb("top_f", [P, WPS, 8])
        gap = sb("gap", [P, WPS])
        tanh = sb("tanh", [P, WPS])
        wtop = sb("wtop", [P, 2, WPS])
        wsel = sb("wsel", [P, WPS, E])
        wf = [sb(f"wf{s}", [P, WPS, E]) for s in range(2)]
        wfT = xT32[0:E, 0, :]
        y = [sb(f"y{s}", [P, WPS, D]) for s in range(2)]
        g32 = sb("g32", [P, 4, WPS * P])
        hid_hi = [sb(f"hid_hi{s}", [P, KH, WPS * P], F16) for s in range(2)]
        hid_lo = [sb(f"hid_lo{s}", [P, KH, WPS * P], F16) for s in range(2)]
        prime = sb("prime", [1, 2, 16])

        def agg(b):
            return psum[:, b, :]

        def f1(c):
            return psum[:, 2 + c % 2, :]

        def f2(tb):
            return psum[:, 4 + tb % 2, 0:D]

        mA, mB = psum[:, 6, :], psum[:, 7, :]

        landed = [sem(f"landed{g}") for g in range(G)]
        batch_ready = sem("batch_ready")
        batch_used = sem("batch_used")
        onehot_free = sem("onehot_free")
        onehot_ready = sem("onehot_ready")
        x_loaded = sem("x_loaded")
        xw_free = sem("xw_free")
        hw_free = sem("hw_free")
        hw_ready = sem("hw_ready")
        agg_ready = sem("agg_ready")
        z_ready = sem("z_ready")
        z_free = sem("z_free")
        mA_free = sem("mA_free")
        mB_free = sem("mB_free")
        to_act = sem("to_act")
        to_dve = sem("to_dve")
        zT_ready = sem("zT_ready")
        aT_ready = sem("aT_ready")
        xn_ready = sem("xn_ready")
        xT_for_dve = sem("xT_for_dve")
        xT_for_pe = sem("xT_for_pe")
        xlo_ready = sem("xlo_ready")
        gap_ready = sem("gap_ready")
        tanh_ready = sem("tanh_ready")
        wf_ready = sem("wf_ready")
        wfT_ready = sem("wfT_ready")
        f1_ready = sem("f1_ready")
        f1_free = sem("f1_free")
        g_ready = sem("g_ready")
        g_free = sem("g_free")
        hid_free = sem("hid_free")
        lo_ready = sem("lo_ready")
        f2_ready = sem("f2_ready")
        f2_free = sem("f2_free")
        y_free = sem("y_free")
        y_done = sem("y_done")
        dev_ready = sem("dev_ready")
        applied = sem("applied")
        act_chain = sem("act_chain")
        pool_step = sem("pool_step")
        w_hi = sem("w_hi")
        stage_free = sem("stage_free")
        pe_chain = sem("pe_chain")
        opeps_ready = sem("opeps_ready")
        x_dma = [sem(f"x_dma{s}") for s in range(2)]
        out_dma = [sem(f"out_dma{s}") for s in range(2)]
        w_dma = [sem(f"w_dma{s}") for s in range(2)]
        x_step = x.rearrange("(i a p) d -> a p i d", i=WPS, p=P)
        out_step = out.rearrange("(i a p) d -> a p i d", i=WPS, p=P)
        rstd_step = rstd0[:].rearrange("p (i a) -> p i a", i=WPS)
        shift_step = shift0[:].rearrange("p (i a) -> p i a", i=WPS)
        block = ctx.enter_context(nc.Block())

        def steps(eng, first_step, body, ffn_only):
            first_step()
            body(1, 0, True, False)
            with eng.Fori(0, (STEPS - 3) // 2) as j:
                for u in range(2):
                    body(2 * j + 2 + u, 1 - u, False, False)
            body(STEPS - 1, 1, False, True)
            ffn_only()

        def second_product(n):
            m = (n - LAG) % NE
            return m // KH, m % KH, n < LAG

        @block.gpsimd
        def _(pool):
            pool.wait_ge(edges_in, 48)
            n_rounds = pool.value_load(rounds[0:1, 1:2], min_val=1, max_val=1 << 20)
            k, tile, left = (pool.alloc_register(n) for n in ("window", "tile", "left"))
            pool.reg_mov(k, 0)
            pool.reg_load(tile, lo_row[0:1, 0:1])
            pool.reg_load(left, nb_row[0:1, 0:1])
            pool.sem_inc(batch_used, G)
            with pool.Fori(0, n_rounds):
                for g in range(G):
                    with pool.If(pool.snap(left) <= 0):
                        pool.reg_add(k, k, 1)
                        at = pool.snap(k, min_val=0, max_val=WINDOWS + 1)
                        pool.reg_load(tile, lo_row[0:1, bass.ds(at, 1)])
                        pool.reg_load(left, nb_row[0:1, bass.ds(at, 1)])
                        pool.nop()
                    pool.wait_ge(batch_used, 1)
                    pool.sem_inc(batch_used, -1)
                    at = pool.snap(tile, min_val=0, max_val=TCOLS - U)
                    pool.tensor_copy(idx_now[:, g, :], src_idx[:, bass.ds(at, U)]).then_inc(pool_step, 1)
                    pool.wait_ge(pool_step, 1)
                    pool.sem_inc(pool_step, -1)
                    for j in range(U):
                        pool.indirect_dma_start(
                            ring[:, (g * U + j) * 2 * D:(g * U + j + 1) * 2 * D], None, table,
                            bass.IndirectOffsetOnAxis(ap=idx_now[:, g, j:j + 1], axis=0)).then_inc(landed[g], 16)
                    pool.reg_add(tile, tile, U)
                    pool.reg_add(left, left, -1)

        @block.sync
        def _(sp):
            n_rounds = sp.value_load(rounds[0:1, 1:2], min_val=1, max_val=1 << 20)
            with sp.Fori(0, n_rounds) as n:
                for g in range(G):
                    sp.wait_ge(landed[g], (n + 1) * (16 * U))
                    sp.wait_ge(onehot_ready, 1)
                    sp.sem_inc(onehot_ready, -1)
                    sp.sem_inc(batch_ready, 1)

        @block.tensor
        def _(pe):
            place = pe.alloc_register("place")
            pe.reg_mov(place, 0)

            left, now = pe.alloc_register("left"), pe.alloc_register("now")

            def sum_batches(bank, n):
                with pe.Fori(0, n):
                    pe.wait_ge(batch_ready, 1)
                    pe.sem_inc(batch_ready, -1)
                    at = pe.snap(pe.snap(place, min_val=0, max_val=G - 1) * (U * P))
                    row = pe.snap(at * (2 * D // P))
                    for j in range(U):
                        ins = pe.matmul(agg(bank), onehot[:, bass.ds(at + j * P, P)],
                                        ring[:, bass.ds(row + j * 2 * D, 2 * D)], start=False, stop=False)
                    ins.then_inc(onehot_free, 1)
                    pe.matmul(agg(bank)[:, 0:ZN], zeros16[:, 0:P], zeros16[:, 0:ZN], start=False, stop=False)\
                      .then_inc(batch_used, 1)
                    pe.reg_add(place, place, 1)
                    pe.reg_alu(place, place, G - 1, ALU.bitwise_and)

            def sum_part(bank, most, first, last):
                if first:
                    pe.matmul(agg(bank), zeros16[:, 0:P], zeros16[:], start=True, stop=False)
                pe.reg_alu(now, left, 1 << 20 if most is None else most, ALU.min)
                pe.reg_alu(left, left, now, ALU.subtract)
                n = pe.snap(now, min_val=0, max_val=1 << 20)
                if first:
                    sum_batches(bank, n)
                else:
                    with pe.If(n > 0):
                        sum_batches(bank, n)
                if last:
                    pe.matmul(agg(bank)[:, 0:ZN], zeros16[:, 0:P], zeros16[:, 0:ZN], start=False, stop=True)\
                      .then_inc(agg_ready, 1)

            def sum_edges(k, bank):
                pe.reg_load(left, nb_row[0:1, bass.ds(k, 1)])
                sum_part(bank, None, True, True)

            def turn_z(p, bank, free):
                pe.wait_ge(z_ready, 1 if p == 0 else 2)
                pe.sem_inc(z_ready, -(1 if p == 0 else 2))
                pe.wait_ge(free, 1)
                pe.sem_inc(free, -1)
                for k in range(KD):
                    for i in range(2):
                        ins = pe.transpose(bank[:, k * D + i * P:k * D + (i + 1) * P],
                                           z[:, 2 * p + i, k * P:(k + 1) * P], ident[:])
                ins.then_inc(pe_chain, 1)
                pe.wait_ge(pe_chain, 1)
                pe.sem_inc(pe_chain, -1)
                pe.sem_inc(to_act, 1)
                pe.sem_inc(z_free, 1)

            def gnn1(p, bank, free):
                pe.wait_ge(zT_ready, 1)
                pe.sem_inc(zT_ready, -1)
                pe.wait_ge(free, 1)
                pe.sem_inc(free, -1)
                for j in range(KD):
                    for k in range(KD):
                        ins = pe.matmul(bank[:, j * D:(j + 1) * D], gW1s[:, k, j * P:(j + 1) * P], zT[:, k, :],
                                        start=(k == 0), stop=(k == KD - 1))
                ins.then_inc(to_act, 1)

            def gnn2(p, bank, free):
                pe.wait_ge(aT_ready, 1)
                pe.sem_inc(aT_ready, -1)
                pe.wait_ge(free, 1)
                pe.sem_inc(free, -1)
                for i in range(2):
                    for k in range(KD):
                        ins = pe.matmul(bank[:, i * D:(i + 1) * D], aT[p][:, k, i * P:(i + 1) * P], gW2s[:, k, :],
                                        start=(k == 0), stop=(k == KD - 1))
                ins.then_inc(to_dve, 1)

            def turn_x(p, bank, free):
                if p == 0:
                    pe.wait_ge(xn_ready, 1)
                    pe.sem_inc(xn_ready, -1)
                pe.wait_ge(free, 1)
                pe.sem_inc(free, -1)
                for k in range(KD):
                    for i in range(2):
                        ins = pe.transpose(bank[:, k * D + i * P:k * D + (i + 1) * P],
                                           r[:, 2 * p + i, k * P:(k + 1) * P], ident[:])
                ins.then_inc(to_act, 1)

            def route(s):
                pe.wait_ge(xT_for_pe, 2)
                pe.sem_inc(xT_for_pe, -2)
                pe.wait_ge(mA_free, 1)
                pe.sem_inc(mA_free, -1)
                for i in range(WPS):
                    for k in range(KD):
                        ins = pe.matmul(mA[:, i * E:(i + 1) * E], xT32[:, k, i * P:(i + 1) * P], fWrs[:, k, :],
                                        start=(k == 0), stop=(k == KD - 1))
                ins.then_inc(to_dve, 1)

            def turn_w(s):
                pe.wait_ge(wf_ready, 1)
                pe.sem_inc(wf_ready, -1)
                pe.wait_ge(mA_free, 1)
                pe.sem_inc(mA_free, -1)
                for i in range(WPS):
                    ins = pe.transpose(mA[0:E, i * P:(i + 1) * P], wf[s][:, i, :], ident[:])
                ins.then_inc(to_dve, 1)

            def out_bias(p, bank, free):
                if p == 0:
                    pe.wait_ge(wfT_ready, 1)
                    pe.sem_inc(wfT_ready, -1)
                pe.wait_ge(free, 1)
                pe.sem_inc(free, -1)
                for i in range(2):
                    ins = pe.matmul(bank[:, i * D:(i + 1) * D], wfT[:, (2 * p + i) * P:(2 * p + i + 1) * P], b2s[:],
                                    start=True, stop=True)
                ins.then_inc(to_dve, 1)

            def expert_in(e, c, s):
                if e == 0 and c == 0:
                    pe.wait_ge(xlo_ready, 2)
                    pe.sem_inc(xlo_ready, -2)
                pe.wait_ge(f1_free, 1)
                pe.sem_inc(f1_free, -1)
                n = 0
                for k in range(KD):
                    for w, v in ((w1hi, xThi), (w1lo, xThi), (w1hi, xTlo)):
                        ins = pe.matmul(f1(c), w[:, e, k, c * P:(c + 1) * P], v[s][:, k, :],
                                        start=(n == 0), stop=(n == 3 * KD - 1))
                        n += 1
                ins.then_inc(f1_ready, 1)

            def expert_out(e, tb):
                pe.wait_ge(f2_free, 1)
                pe.sem_inc(f2_free, -1)
                cols = slice(tb * P, (tb + 1) * P)
                n = 0
                for k in range(KH):
                    for v, w in ((hid_hi, w2hi), (hid_hi, w2lo), (hid_lo, w2hi)):
                        ins = pe.matmul(f2(tb), v[e % 2][:, k, cols], w[:, e, k, :],
                                        start=(n == 0), stop=(n == 3 * KH - 1))
                        n += 1
                ins.then_inc(f2_ready, 1)

            def first_step():
                pe.wait_ge(opeps_ready, 1)
                pe.sem_inc(opeps_ready, -1)
                pe.sem_inc(mA_free, 1)
                pe.sem_inc(mB_free, 1)
                sum_edges(0, 0)
                sum_edges(1, 1)
                pe.wait_ge(z_ready, 1)
                pe.sem_inc(z_ready, -1)
                sum_edges(2, 0)
                turn_z(0, mA, mA_free)
                gnn1(0, mA, mA_free)
                gnn2(0, mA, mA_free)
                sum_edges(3, 1)
                turn_z(1, mB, mB_free)
                gnn1(1, mB, mB_free)
                gnn2(1, mB, mB_free)
                sum_edges(4, 0)
                sum_edges(5, 1)
                turn_x(0, mA, mA_free)
                turn_x(1, mB, mB_free)

            def experts(n, s, first):
                if n < NE and n % KH > 0:
                    expert_in(n // KH, n % KH, s)
                if n % KH < 2 and n < NE + 2 and not (first and n < KH):
                    count = (1, KH - 1)[n % KH]
                    pe.wait_ge(lo_ready, count)
                    pe.sem_inc(lo_ready, -count)
                    pe.sem_inc(g_free, count)
                if not (first and n < LAG):
                    e, tb, _ = second_product(n)
                    expert_out(e, tb)
                if n < NE and n % KH == 0:
                    expert_in(n // KH, n % KH, s)

            def body(b, s, first, last):
                for n in range(NE):
                    experts(n, s, first)
                    if n == 0:
                        route(s)
                    if n == 1:
                        pe.wait_ge(z_ready, 1)
                        pe.sem_inc(z_ready, -1)
                        sum_edges(4 * b + 2, 0)
                    if n == 2:
                        turn_z(0, mB, mB_free)
                    if n == 3:
                        turn_w(s)
                    if n == 4:
                        gnn1(0, mB, mB_free)
                        sum_edges(4 * b + 3, 1)
                    if n == 5:
                        out_bias(0, mA, mA_free)
                    if n == 6:
                        gnn2(0, mB, mB_free)
                    if n == 7:
                        out_bias(1, mA, mA_free)
                    if n == 8:
                        turn_z(1, mB, mB_free)
                    if n == 9:
                        gnn1(1, mB, mB_free)
                    if n == 11:
                        gnn2(1, mB, mB_free)
                    for i, (at, most) in enumerate(PARTS):
                        if n == at and not last:
                            if i == 0:
                                pe.reg_load(left, nb_row[0:1, bass.ds(4 * b + 4, 1)])
                            sum_part(0, most, i == 0, most is None)
                    if n == 30 and not last:
                        sum_edges(4 * b + 5, 1)
                    if n == 28:
                        turn_x(0, mA, mA_free)
                    if n == 29:
                        turn_x(1, mB, mB_free)

            def ffn_only():
                s = (STEPS - 1) % 2
                for n in range(NE + LAG):
                    experts(n, s, False)
                    if n == 0:
                        route(s)
                    if n == 3:
                        turn_w(s)
                    if n == 5:
                        out_bias(0, mA, mA_free)
                    if n == 7:
                        out_bias(1, mA, mA_free)

            steps(pe, first_step, body, ffn_only)

        @block.scalar
        def _(act):
            w_pieces = [(fW1[e].rearrange("(k p) h -> p k h", p=P), KD) for e in range(E)] + \
                       [(fW2[e].rearrange("(k p) d -> p k d", p=P), KH) for e in range(E)]

            def load_x(b, s):
                act.dma_start(xw[s][:], x_step[STEPS - 1 - b]).then_inc(x_dma[s], 16)

            def norm_x(b, s, p):
                if p == 0:
                    act.wait_ge(x_dma[s], 16)
                    act.sem_inc(x_dma[s], -16)
                act.wait_ge(hw_free, 1)
                act.sem_inc(hw_free, -1)
                for i in (2 * p, 2 * p + 1):
                    a = bass.ds(STEPS - 1 - b, 1)
                    ins = act.activation(hw[:, i, :], xw[s][:, i, :], ACT.Identity, bias=shift_step[:, i, a],
                                         scale=rstd_step[:, i, a])
                ins.then_inc(hw_ready, 1)

            def copy_zT(bank, free):
                act.wait_ge(to_act, 1)
                act.sem_inc(to_act, -1)
                act.activation(zT[:].rearrange("p k n -> p (k n)"), bank, ACT.Identity).then_inc(act_chain, 1)
                act.wait_ge(act_chain, 1)
                act.sem_inc(act_chain, -1)
                act.sem_inc(free, 1)
                act.sem_inc(zT_ready, 1)

            def relu_a(p, bank, free):
                act.wait_ge(to_act, 1)
                act.sem_inc(to_act, -1)
                for j in range(KD):
                    ins = act.activation(aT[p][:, j, :], bank[:, j * D:(j + 1) * D], ACT.Relu, bias=gb1s[:, j:j + 1])
                ins.then_inc(act_chain, 1)
                act.wait_ge(act_chain, 1)
                act.sem_inc(act_chain, -1)
                act.sem_inc(free, 1)
                act.sem_inc(aT_ready, 1)

            def copy_xT(p, s, bank, free):
                act.wait_ge(to_act, 1)
                act.sem_inc(to_act, -1)
                cols = slice(2 * p * P, 2 * (p + 1) * P)
                for k in range(KD):
                    ins = act.activation(xT32[:, k, cols], bank[:, k * D:(k + 1) * D], ACT.Identity,
                                         bias=fbs[:, k:k + 1], scale=fgs[:, k:k + 1])
                ins.then_inc(act_chain, 1)
                act.wait_ge(act_chain, 1)
                act.sem_inc(act_chain, -1)
                act.sem_inc(free, 1)
                act.activation(xThi[s][:, :, cols], xT32[:, :, cols], ACT.Identity).then_inc(act_chain, 1)
                act.wait_ge(act_chain, 1)
                act.sem_inc(act_chain, -1)
                act.sem_inc(xT_for_dve, 1)
                act.sem_inc(xT_for_pe, 1)

            def apply(dst, v, ready):
                act.wait_ge(dev_ready, 1)
                act.sem_inc(dev_ready, -1)
                for i in range(WPS):
                    ins = act.activation(dst[:, i, :], v[:, i, :], ACT.Identity, bias=small[:, 4, i:i + 1],
                                         scale=small[:, 3, i:i + 1])
                ins.then_inc(ready, 1)

            def gate_tanh():
                act.wait_ge(gap_ready, 1)
                act.sem_inc(gap_ready, -1)
                act.activation(tanh[:], gap[:], ACT.Tanh, scale=0.5).then_inc(tanh_ready, 1)

            def gelu(e, c):
                act.wait_ge(f1_ready, 1)
                act.sem_inc(f1_ready, -1)
                act.wait_ge(g_free, 1)
                act.sem_inc(g_free, -1)
                if c == 0:
                    act.wait_ge(hid_free, 1)
                    act.sem_inc(hid_free, -1)
                for dst in (g32[:, c, :], hid_hi[e % 2][:, c, :]):
                    ins = act.activation(dst, f1(c), ACT.Gelu, bias=fb1s[:, e * KH + c:e * KH + c + 1],
                                         scale=1.0 / WSCALE)
                ins.then_inc(act_chain, 1)
                act.wait_ge(act_chain, 1)
                act.sem_inc(act_chain, -1)
                act.sem_inc(f1_free, 1)
                act.sem_inc(g_ready, 1)

            def store_y(b, s):
                act.wait_ge(y_done, 1)
                act.sem_inc(y_done, -1)
                act.dma_start(out_step[STEPS - 1 - b], y[s][:]).then_inc(out_dma[s], 16)

            def y_is_free(s):
                act.wait_ge(out_dma[s], 16)
                act.sem_inc(out_dma[s], -16)
                act.sem_inc(y_free, 1)

            def first_step():
                for s in range(2):
                    act.dma_start(prime[:, s, :], x[0:1, 0:16]).then_inc(out_dma[s], 16)
                load_x(0, 0)
                load_x(1, 1)
                act.sem_inc(hw_free, 2)
                act.sem_inc(f1_free, 2)
                norm_x(0, 0, 0)
                norm_x(0, 0, 1)
                for n, (source, kk) in enumerate(w_pieces):
                    stage = g32[:, 2 * (n % 2):2 * (n % 2) + 2, :].rearrange("p a n -> p (a n)")
                    if n >= 2:
                        act.wait_ge(stage_free, 1)
                        act.sem_inc(stage_free, -1)
                    act.dma_start(stage.rearrange("p (k h) -> p k h", k=kk), source).then_inc(w_dma[n % 2], 16)
                    if n >= 1:
                        weight_hi(n - 1)
                weight_hi(len(w_pieces) - 1)
                act.wait_ge(stage_free, 2)
                act.sem_inc(stage_free, -2)
                act.sem_inc(g_free, 4)
                copy_zT(mA, mA_free)
                relu_a(0, mA, mA_free)
                copy_zT(mB, mB_free)
                relu_a(1, mB, mB_free)
                norm_x(1, 1, 0)
                y_is_free(0)
                apply(t, r, applied)
                apply(t, y[0], applied)
                apply(r, t, xn_ready)
                copy_xT(0, 0, mA, mA_free)
                copy_xT(1, 0, mB, mB_free)

            def weight_hi(n):
                stage = g32[:, 2 * (n % 2):2 * (n % 2) + 2, :].rearrange("p a n -> p (a n)")
                dst = (w1hi if n < E else w2hi)[:, n % E, :, :].rearrange("p k h -> p (k h)")
                act.wait_ge(w_dma[n % 2], 16)
                act.sem_inc(w_dma[n % 2], -16)
                act.activation(dst, stage, ACT.Copy, scale=WSCALE).then_inc(w_hi, 1)

            def body(b, s, first, last):
                for n in range(NE):
                    gelu(n // KH, n % KH)
                    if n == 0:
                        if not last:
                            act.wait_ge(xw_free, 1)
                            act.sem_inc(xw_free, -1)
                            load_x(b + 1, s)
                        norm_x(b, 1 - s, 1)
                    if n == 1:
                        gate_tanh()
                    if n == 6 and not first:
                        store_y(b - 2, 1 - s)
                    if n == 2:
                        copy_zT(mB, mB_free)
                    if n == 4:
                        relu_a(0, mB, mB_free)
                    if n == 8:
                        copy_zT(mB, mB_free)
                    if n == 9:
                        relu_a(1, mB, mB_free)
                    if n == 13 and not last:
                        norm_x(b + 1, s, 0)
                    if n == 14:
                        y_is_free(1 - s)
                    if n == 15:
                        apply(t, r, applied)
                    if n == 22:
                        apply(t, y[1 - s], applied)
                    if n == 27:
                        apply(r, t, xn_ready)
                    if n == 28:
                        copy_xT(0, 1 - s, mA, mA_free)
                    if n == 29:
                        copy_xT(1, 1 - s, mB, mB_free)

            def ffn_only():
                s = (STEPS - 1) % 2
                for n in range(NE):
                    gelu(n // KH, n % KH)
                    if n == 2:
                        gate_tanh()
                    if n == 6:
                        store_y(STEPS - 2, 1 - s)
                store_y(STEPS - 1, s)
                for s in range(2):
                    act.wait_ge(out_dma[s], 16)

            steps(act, first_step, body, ffn_only)

        @block.vector
        def _(dve):
            place, tile = dve.alloc_register("place"), dve.alloc_register("tile")
            dve.reg_mov(place, 0)

            left, now = dve.alloc_register("left"), dve.alloc_register("now")

            def open_window(k, half):
                dve.reg_load(tile, lo_row[0:1, bass.ds(k, 1)])
                dve.reg_load(left, nb_row[0:1, bass.ds(k, 1)])
                dve.tensor_scalar(iota_k[:, half, :], iota16[:], base[:, bass.ds(k, 1)], None, ALU.add).then_inc(chain, 1)
                dve.wait_ge(chain, 1)
                dve.sem_inc(chain, -1)

            def onehot_batches(half, n):
                with dve.Fori(0, n):
                    dve.wait_ge(onehot_free, 1)
                    dve.sem_inc(onehot_free, -1)
                    to = dve.snap(dve.snap(place, min_val=0, max_val=G - 1) * (U * P))
                    at = dve.snap(tile, min_val=0, max_val=TCOLS - U)
                    dve.tensor_tensor(onehot[:, bass.ds(to, U * P)].rearrange("p (t e) -> p t e", t=U),
                                      iota_k[:, half, :].unsqueeze(1).broadcast_to([P, U, P]),
                                      dst_f[:, bass.ds(at, U)].unsqueeze(2).broadcast_to([P, U, P]),
                                      ALU.is_equal).then_inc(onehot_ready, 1)
                    dve.reg_add(place, place, 1)
                    dve.reg_alu(place, place, G - 1, ALU.bitwise_and)
                    dve.reg_add(tile, tile, U)

            def onehots_part(half, most, first):
                dve.reg_alu(now, left, 1 << 20 if most is None else most, ALU.min)
                dve.reg_alu(left, left, now, ALU.subtract)
                n = dve.snap(now, min_val=0, max_val=1 << 20)
                if first:
                    onehot_batches(half, n)
                else:
                    with dve.If(n > 0):
                        onehot_batches(half, n)

            def onehots(k, half):
                open_window(k, half)
                onehots_part(half, None, True)

            def add_z(i):
                if i % 2 == 0:
                    dve.wait_ge(hw_ready, 1)
                    dve.sem_inc(hw_ready, -1)
                    dve.wait_ge(z_free, 1)
                    dve.sem_inc(z_free, -1)
                dve.wait_ge(agg_ready, 1)
                dve.sem_inc(agg_ready, -1)
                dve.scalar_tensor_tensor(out=z[:, i, :], in0=hw[:, i, :], scalar=opeps[:, 0:1],
                                         in1=agg(i % 2)[:, 0:D], op0=ALU.mult, op1=ALU.add).then_inc(chain, 1)
                dve.wait_ge(chain, 1)
                dve.sem_inc(chain, -1)
                dve.tensor_tensor(z[:, i, :], z[:, i, :], agg(i % 2)[:, D:2 * D], ALU.add).then_inc(z_ready, 1)

            def residual(p, bank, free):
                two = slice(2 * p, 2 * p + 2)
                dve.tensor_tensor(r[:, two, :], hw[:, two, :], gb2s[:].unsqueeze(1).broadcast_to([P, 2, D]),
                                  ALU.add).then_inc(chain, 1)
                dve.wait_ge(chain, 1)
                dve.sem_inc(chain, -1)
                dve.sem_inc(hw_free, 1)
                dve.wait_ge(to_dve, 1)
                dve.sem_inc(to_dve, -1)
                dve.tensor_tensor(r[:, two, :], r[:, two, :], bank.rearrange("p (i d) -> p i d", i=2),
                                  ALU.add).then_inc(chain, 1)
                dve.wait_ge(chain, 1)
                dve.sem_inc(chain, -1)
                dve.sem_inc(free, 1)

            rstd, shift = small[:, 3, 0:WPS], small[:, 4, 0:WPS]

            def moments(v):
                for i in range(WPS):
                    ins = dve.bn_stats(bstats[:, i, :], v[:, i, :])
                ins.then_inc(chain, 1)
                dve.wait_ge(chain, 1)
                dve.sem_inc(chain, -1)
                for i in range(WPS):
                    ins = dve.bn_aggr(bmv[:, i, :], bstats[:, i, :])
                ins.then_inc(chain, 1)
                dve.wait_ge(chain, 1)
                dve.sem_inc(chain, -1)

            tmp = [small[:, n, 0:WPS] for n in range(3)]

            def deviations_1():
                rsqrt_seed(dve, chain, rstd, bmv[:, :, 1], tmp)

            def deviations_2():
                newton(dve, chain, rstd, tmp)
                newton(dve, chain, rstd, tmp)
                dve.scalar_tensor_tensor(out=shift, in0=bmv[:, :, 0], scalar=-1.0, in1=rstd,
                                         op0=ALU.mult, op1=ALU.mult).then_inc(dev_ready, 1)

            def over_i(a):
                return a.unsqueeze(1).broadcast_to([P, WPS, D])

            def ln_gamma():
                dve.wait_ge(applied, 1)
                dve.sem_inc(applied, -1)
                dve.tensor_tensor(t[:], t[:], over_i(ggs[:]), ALU.mult).then_inc(chain, 1)
                dve.wait_ge(chain, 1)
                dve.sem_inc(chain, -1)

            def ln_beta():
                dve.tensor_tensor(t[:], t[:], over_i(gbs[:]), ALU.add).then_inc(chain, 1)
                dve.wait_ge(chain, 1)
                dve.sem_inc(chain, -1)

            def add_x(s):
                dve.wait_ge(y_free, 1)
                dve.sem_inc(y_free, -1)
                dve.scalar_tensor_tensor(out=y[s][:], in0=t[:], scalar=0.0, in1=xw[s][:], op0=ALU.max,
                                         op1=ALU.add).then_inc(chain, 1)
                dve.wait_ge(chain, 1)
                dve.sem_inc(chain, -1)
                dve.sem_inc(xw_free, 1)

            def second_moments():
                dve.wait_ge(applied, 1)
                dve.sem_inc(applied, -1)
                moments(t)

            def split_xT(p, s):
                dve.wait_ge(xT_for_dve, 1)
                dve.sem_inc(xT_for_dve, -1)
                cols = slice(2 * p * P, 2 * (p + 1) * P)
                dve.tensor_tensor(xTlo[s][:, :, cols], xT32[:, :, cols], xThi[s][:, :, cols], ALU.subtract)\
                   .then_inc(xlo_ready, 1)

            def top_two():
                dve.wait_ge(to_dve, 1)
                dve.sem_inc(to_dve, -1)
                dve.tensor_tensor(logit[:], mA[:, 0:WPS * E].rearrange("p (i e) -> p i e", i=WPS),
                                  fbrs[:].unsqueeze(1).broadcast_to([P, WPS, E]), ALU.add).then_inc(chain, 1)
                dve.wait_ge(chain, 1)
                dve.sem_inc(chain, -1)
                dve.sem_inc(mA_free, 1)
                for i in range(WPS):
                    ins = dve.max(top[:, i, :], logit[:, i, :])
                ins.then_inc(chain, 1)
                dve.wait_ge(chain, 1)
                dve.sem_inc(chain, -1)
                dve.tensor_tensor(gap[:], top[:, :, 0], top[:, :, 1], ALU.subtract).then_inc(gap_ready, 1)
                for i in range(WPS):
                    ins = dve.max_index(top_i[:, i, :], top[:, i, :], logit[:, i, :])
                ins.then_inc(chain, 1)
                dve.wait_ge(chain, 1)
                dve.sem_inc(chain, -1)
                dve.tensor_copy(top_f[:], top_i[:]).then_inc(chain, 1)
                dve.wait_ge(chain, 1)
                dve.sem_inc(chain, -1)

            def gates(s):
                dve.wait_ge(tanh_ready, 1)
                dve.sem_inc(tanh_ready, -1)
                half = 0.5 / WSCALE
                dve.tensor_scalar(wtop[:, 0, :], tanh[:], half, half, ALU.mult, ALU.add)
                dve.tensor_scalar(wtop[:, 1, :], tanh[:], -half, half, ALU.mult, ALU.add).then_inc(chain, 1)
                dve.wait_ge(chain, 1)
                dve.sem_inc(chain, -1)
                for n, dst in enumerate((wf[s], wsel)):
                    for i in range(WPS):
                        ins = dve.tensor_scalar(dst[:, i, :], iota8[:], top_f[:, i, n:n + 1], wtop[:, n, i:i + 1],
                                                ALU.is_equal, ALU.mult)
                ins.then_inc(chain, 1)
                dve.wait_ge(chain, 1)
                dve.sem_inc(chain, -1)
                dve.tensor_tensor(wf[s][:], wf[s][:], wsel[:], ALU.add).then_inc(chain, 1)
                dve.wait_ge(chain, 1)
                dve.sem_inc(chain, -1)
                dve.sem_inc(wf_ready, 1)

            def copy_wfT():
                dve.wait_ge(to_dve, 1)
                dve.sem_inc(to_dve, -1)
                dve.tensor_copy(wfT, mA[0:E, :]).then_inc(chain, 1)
                dve.wait_ge(chain, 1)
                dve.sem_inc(chain, -1)
                dve.sem_inc(mA_free, 1)
                dve.sem_inc(wfT_ready, 1)

            def start_y(p, s, bank, free):
                dve.wait_ge(to_dve, 1)
                dve.sem_inc(to_dve, -1)
                two = slice(2 * p, 2 * p + 2)
                dve.tensor_tensor(y[s][:, two, :], y[s][:, two, :], bank.rearrange("p (i d) -> p i d", i=2),
                                  ALU.add).then_inc(chain, 1)
                dve.wait_ge(chain, 1)
                dve.sem_inc(chain, -1)
                dve.sem_inc(free, 1)

            def rest_of_gelu(e, c):
                dve.wait_ge(g_ready, 1)
                dve.sem_inc(g_ready, -1)
                dve.tensor_tensor(hid_lo[e % 2][:, c, :], g32[:, c, :], hid_hi[e % 2][:, c, :],
                                  ALU.subtract).then_inc(lo_ready, 1)

            def add_y(e, tb, s):
                dve.wait_ge(f2_ready, 1)
                dve.sem_inc(f2_ready, -1)
                if tb == WPS - 1:
                    dve.sem_inc(hid_free, 1)
                ins = dve.scalar_tensor_tensor(out=y[s][:, tb, :], in0=f2(tb), scalar=wf[s][:, tb, e:e + 1],
                                               in1=y[s][:, tb, :], op0=ALU.mult, op1=ALU.add)
                if (e, tb) == (E - 1, WPS - 1):
                    ins.then_inc(chain, 1)
                    dve.wait_ge(chain, 1)
                    dve.sem_inc(chain, -1)
                    dve.sem_inc(f2_free, 1)
                    dve.sem_inc(y_done, 1)
                elif e == 0:
                    ins.then_inc(chain, 1)
                    dve.wait_ge(chain, 1)
                    dve.sem_inc(chain, -1)
                    dve.sem_inc(f2_free, 1)
                else:
                    ins.then_inc(f2_free, 1)

            def first_step():
                dve.sem_inc(onehot_free, G)
                dve.sem_inc(z_free, 2)
                dve.sem_inc(f2_free, 2)
                dve.sem_inc(hid_free, 2)
                dve.tensor_scalar(b2s[:], fb2s[:], WSCALE, None, ALU.mult)
                dve.tensor_scalar(opeps[:], eps1[:], 1.0, None, ALU.add).then_inc(chain, 1)
                dve.wait_ge(chain, 1)
                dve.sem_inc(chain, -1)
                dve.sem_inc(opeps_ready, 1)
                onehots(0, 0)
                for n in range(2 * E):
                    if n == 4:
                        onehots(1, 1)
                    if n == 8:
                        add_z(0)
                        onehots(2, 0)
                    if n == 12:
                        add_z(1)
                        onehots(3, 1)
                    stage = g32[:, 2 * (n % 2):2 * (n % 2) + 2, :].rearrange("p a n -> p (a n)")
                    hi, lo = ((w1hi, w1lo) if n < E else (w2hi, w2lo))
                    dve.wait_ge(w_hi, 1)
                    dve.sem_inc(w_hi, -1)
                    dve.scalar_tensor_tensor(out=lo[:, n % E].rearrange("p k h -> p (k h)"), in0=stage, scalar=WSCALE,
                                             in1=hi[:, n % E].rearrange("p k h -> p (k h)"), op0=ALU.mult,
                                             op1=ALU.subtract).then_inc(stage_free, 1)
                add_z(2)
                residual(0, mA, mA_free)
                add_z(3)
                residual(1, mB, mB_free)
                onehots(4, 0)
                onehots(5, 1)
                moments(r)
                deviations_1()
                deviations_2()
                ln_gamma()
                ln_beta()
                add_x(0)
                moments(y[0])
                deviations_1()
                deviations_2()
                second_moments()
                deviations_1()
                deviations_2()
                add_z(0)
                add_z(1)
                split_xT(0, 0)
                split_xT(1, 0)
                onehots(6, 0)

            def experts(n, s, first):
                if not (first and n < LAG):
                    e, tb, before = second_product(n)
                    add_y(e, tb, 1 - s if before else s)
                if n < NE:
                    rest_of_gelu(n // KH, n % KH)

            def body(b, s, first, last):
                for n in range(NE):
                    experts(n, s, first)
                    if n == 0:
                        top_two()
                    if n == 1:
                        gates(s)
                    if n == 2:
                        onehots(4 * b + 3, 1)
                    if n == 3:
                        add_z(2)
                        copy_wfT()
                    if n == 5:
                        start_y(0, s, mA, mA_free)
                    if n == 6:
                        residual(0, mB, mB_free)
                    if n == 7:
                        start_y(1, s, mA, mA_free)
                        add_z(3)
                    if n == 11:
                        residual(1, mB, mB_free)
                    if n == 12:
                        moments(r)
                    if n == 13:
                        deviations_1()
                    if n == 14:
                        deviations_2()
                    if n == 16:
                        ln_gamma()
                        ln_beta()
                    if n == 17:
                        add_x(1 - s)
                    if n == 18:
                        moments(y[1 - s])
                    if n == 19:
                        deviations_1()
                    if n == 20:
                        deviations_2()
                    if n == 23:
                        second_moments()
                    if n == 24:
                        deviations_1()
                    if n == 25:
                        deviations_2()
                    if n == 30:
                        split_xT(0, 1 - s)
                    if n == 31:
                        split_xT(1, 1 - s)
                    if not last:
                        for i, (at, most) in enumerate(PARTS):
                            if n == at - 2:
                                if i == 0:
                                    open_window(4 * b + 4, 0)
                                onehots_part(0, most, i == 0)
                        if n == 29:
                            add_z(0)
                        if n == 28:
                            onehots(4 * b + 5, 1)
                        if n == 31:
                            add_z(1)
                        if n == 31:
                            onehots(4 * b + 6, 0)

            def ffn_only():
                dve.sem_inc(onehot_ready, G)
                s = (STEPS - 1) % 2
                for n in range(NE + LAG):
                    experts(n, s, False)
                    if n == 0:
                        top_two()
                    if n == 2:
                        gates(s)
                    if n == 3:
                        copy_wfT()
                    if n == 5:
                        start_y(0, s, mA, mA_free)
                    if n == 7:
                        start_y(1, s, mA, mA_free)

            steps(dve, first_step, body, ffn_only)


def kernel(**inputs):
    import numpy as np
    import concourse.bacc as bacc
    from concourse.bass_utils import run_bass_kernel_spmd

    nodes = inputs["x"].shape[0]
    x = np.zeros((ROWS, D), np.float32)
    x[:nodes] = inputs["x"]
    src = np.zeros(TPAD * P, np.int32)
    src[:EDGES] = inputs["src"]
    dst = np.full(TPAD * P, NOWHERE, np.int32)
    dst[:EDGES] = inputs["dst"]
    arrays = {
        "x": x,
        "src_cols": np.ascontiguousarray(src.reshape(TPAD, P)[:TCOLS].T),
        "dst_cols": np.ascontiguousarray(dst.reshape(TPAD, P)[:TCOLS].T),
        "dst_rows": dst.reshape(TPAD, P),
    }
    for name in ("gnn_W1", "gnn_b1", "gnn_W2", "gnn_b2", "gnn_eps", "gnn_gamma", "gnn_beta", "ffn_gamma", "ffn_beta",
                 "ffn_Wr", "ffn_br", "ffn_W1", "ffn_b1", "ffn_W2", "ffn_b2"):
        a = np.ascontiguousarray(inputs["L0_" + name])
        arrays[name] = a.reshape(1) if a.ndim == 0 else a
    nc = bacc.Bacc("TRN2", target_bir_lowering=False, num_devices=1)
    args = [nc.dram_tensor("in_" + n, a.shape, mybir.dt.from_np(a.dtype), kind="ExternalInput").ap()
            for n, a in arrays.items()]
    out = nc.dram_tensor("out", (ROWS, D), F32, kind="ExternalOutput").ap()
    gnn_moe_kernel(nc, *args, out)
    r = run_bass_kernel_spmd(nc, [{"in_" + n: a for n, a in arrays.items()}], core_ids=[0])
    return r.results[0]["out"][:nodes]
```
